# Optimizing a Trainium2 kernel written in Bass

```python
import numpy as np
import jax
import jax.numpy as jnp

def _softmax(x, axis=-1):
    return jax.nn.softmax(x, axis=axis)

def _gelu(x):
    return jax.nn.gelu(x, approximate=True)

def _silu(x):
    return jax.nn.silu(x)

def _sigmoid(x):
    return jax.nn.sigmoid(x)

def _layernorm(x, axis=-1, eps=1e-05):
    m = jnp.mean(x, axis=axis, keepdims=True)
    v = jnp.var(x, axis=axis, keepdims=True)
    return (x - m) / jnp.sqrt(v + eps)

def _scatter_add(tgt, idx, src, axis=0):
    return tgt.at[idx].add(src)

def _segment_sum(src, seg, n):
    return jax.ops.segment_sum(src, seg, n)
kernel_name = 'mk_macaron_d1_jaxref_r8_6ac093'

def setup_inputs(seed: int=0):
    np.random.seed(seed)
    _w = jnp.asarray

    def _L0_attn_setup():
        import jax, jax.numpy as jnp
        import numpy as np
        C = 256
        H = 4 * C
        NEG_INF = -1e+38

        def layer_norm(x, w, b, eps=1e-05):
            mu = jnp.mean(x, axis=-1, keepdims=True)
            var = jnp.var(x, axis=-1, keepdims=True)
            return (x - mu) * jax.lax.rsqrt(var + eps) * w + b

        def time_shift(x):
            return jnp.pad(x, ((0, 0), (1, 0), (0, 0)))[:, :-1]

        def wkv(w_decay, u_first, k, v):
            w = -jnp.exp(w_decay)
            B = k.shape[0]
            kT = jnp.swapaxes(k, 0, 1)
            vT = jnp.swapaxes(v, 0, 1)

            def step(carry, kv_t):
                aa, bb, pp = carry
                kt, vt = kv_t
                ww = u_first + kt
                p = jnp.maximum(pp, ww)
                e1 = jnp.exp(pp - p)
                e2 = jnp.exp(ww - p)
                y = (e1 * aa + e2 * vt) / (e1 * bb + e2)
                ww2 = pp + w
                p2 = jnp.maximum(ww2, kt)
                e1b = jnp.exp(ww2 - p2)
                e2b = jnp.exp(kt - p2)
                return ((e1b * aa + e2b * vt, e1b * bb + e2b, p2), y)
            init = (jnp.zeros((B, C), k.dtype), jnp.zeros((B, C), k.dtype), jnp.full((B, C), NEG_INF, k.dtype))
            _, yT = jax.lax.scan(step, init, (kT, vT))
            return jnp.swapaxes(yT, 0, 1)
        key = jax.random.key(seed)
        ks = jax.random.split(key, 16)
        s = lambda n: 1.0 / np.sqrt(n)
        inp = {'x': jax.random.normal(ks[0], (8, 256, C), jnp.float32), 'ln1_w': jnp.ones((C,)), 'ln1_b': jnp.zeros((C,)), 'ln2_w': jnp.ones((C,)), 'ln2_b': jnp.zeros((C,)), 'time_decay': jax.random.normal(ks[1], (C,)) * 0.5, 'time_first': jax.random.normal(ks[2], (C,)) * 0.5, 'tmk': jax.random.uniform(ks[3], (C,)), 'tmv': jax.random.uniform(ks[4], (C,)), 'tmr': jax.random.uniform(ks[5], (C,)), 'Wk': jax.random.normal(ks[6], (C, C)) * s(C), 'Wv': jax.random.normal(ks[7], (C, C)) * s(C), 'Wr': jax.random.normal(ks[8], (C, C)) * s(C), 'Wo': jax.random.normal(ks[9], (C, C)) * s(C), 'cmk': jax.random.uniform(ks[10], (C,)), 'cmr': jax.random.uniform(ks[11], (C,)), 'Wck': jax.random.normal(ks[12], (H, C)) * s(C), 'Wcv': jax.random.normal(ks[13], (C, H)) * s(H), 'Wcr': jax.random.normal(ks[14], (C, C)) * s(C)}
        return inp
    _L0_attn_in = _L0_attn_setup()

    def _L0_ffn_setup():
        import jax, jax.numpy as jnp
        import numpy as np
        HIDDEN = 256
        INTER = 688
        LUT_SIZE = 16

        def _ghost_linear(x, idx, lut):
            w = lut[idx]
            return jnp.einsum('bsh,oh->bso', x, w)
        key = jax.random.key(seed)
        k_x, k_lut, k_g, k_u, k_d = jax.random.split(key, 5)
        x = jax.random.normal(k_x, (2, 512, HIDDEN), dtype=jnp.float32)
        lut = jax.random.normal(k_lut, (LUT_SIZE,), dtype=jnp.float32) * 0.02
        gate_idx = jax.random.randint(k_g, (INTER, HIDDEN), 0, LUT_SIZE, dtype=jnp.int32)
        up_idx = jax.random.randint(k_u, (INTER, HIDDEN), 0, LUT_SIZE, dtype=jnp.int32)
        down_idx = jax.random.randint(k_d, (HIDDEN, INTER), 0, LUT_SIZE, dtype=jnp.int32)
        return {'x': x, 'lut': lut, 'gate_idx': gate_idx, 'up_idx': up_idx, 'down_idx': down_idx}
    _L0_ffn_in = _L0_ffn_setup()
    _d = {'L0_attn_x': _L0_attn_in['x'], 'L0_attn_ln1_w': _L0_attn_in['ln1_w'], 'L0_attn_ln1_b': _L0_attn_in['ln1_b'], 'L0_attn_ln2_w': _L0_attn_in['ln2_w'], 'L0_attn_ln2_b': _L0_attn_in['ln2_b'], 'L0_attn_time_decay': _L0_attn_in['time_decay'], 'L0_attn_time_first': _L0_attn_in['time_first'], 'L0_attn_tmk': _L0_attn_in['tmk'], 'L0_attn_tmv': _L0_attn_in['tmv'], 'L0_attn_tmr': _L0_attn_in['tmr'], 'L0_attn_Wk': _L0_attn_in['Wk'], 'L0_attn_Wv': _L0_attn_in['Wv'], 'L0_attn_Wr': _L0_attn_in['Wr'], 'L0_attn_Wo': _L0_attn_in['Wo'], 'L0_attn_cmk': _L0_attn_in['cmk'], 'L0_attn_cmr': _L0_attn_in['cmr'], 'L0_attn_Wck': _L0_attn_in['Wck'], 'L0_attn_Wcv': _L0_attn_in['Wcv'], 'L0_attn_Wcr': _L0_attn_in['Wcr'], 'L0_ffn_lut': _L0_ffn_in['lut'], 'L0_ffn_gate_idx': _L0_ffn_in['gate_idx'], 'L0_ffn_up_idx': _L0_ffn_in['up_idx'], 'L0_ffn_down_idx': _L0_ffn_in['down_idx']}
    _x0 = _d['L0_attn_x']
    _d['L0_attn_x'] = jax.random.normal(jax.random.fold_in(jax.random.key(seed), 1), (1, 2048, 256), dtype=_x0.dtype)
    del _x0
    return _d

def reference(L0_attn_x, L0_attn_ln1_w, L0_attn_ln1_b, L0_attn_ln2_w, L0_attn_ln2_b, L0_attn_time_decay, L0_attn_time_first, L0_attn_tmk, L0_attn_tmv, L0_attn_tmr, L0_attn_Wk, L0_attn_Wv, L0_attn_Wr, L0_attn_Wo, L0_attn_cmk, L0_attn_cmr, L0_attn_Wck, L0_attn_Wcv, L0_attn_Wcr, L0_ffn_lut, L0_ffn_gate_idx, L0_ffn_up_idx, L0_ffn_down_idx):

    def _L0_attn_ref(x, ln1_w, ln1_b, ln2_w, ln2_b, time_decay, time_first, tmk, tmv, tmr, Wk, Wv, Wr, Wo, cmk, cmr, Wck, Wcv, Wcr):
        import jax, jax.numpy as jnp
        import numpy as np
        C = 256
        H = 4 * C
        NEG_INF = -1e+38

        def layer_norm(x, w, b, eps=1e-05):
            mu = jnp.mean(x, axis=-1, keepdims=True)
            var = jnp.var(x, axis=-1, keepdims=True)
            return (x - mu) * jax.lax.rsqrt(var + eps) * w + b

        def time_shift(x):
            return jnp.pad(x, ((0, 0), (1, 0), (0, 0)))[:, :-1]

        def wkv(w_decay, u_first, k, v):
            w = -jnp.exp(w_decay)
            B = k.shape[0]
            kT = jnp.swapaxes(k, 0, 1)
            vT = jnp.swapaxes(v, 0, 1)

            def step(carry, kv_t):
                aa, bb, pp = carry
                kt, vt = kv_t
                ww = u_first + kt
                p = jnp.maximum(pp, ww)
                e1 = jnp.exp(pp - p)
                e2 = jnp.exp(ww - p)
                y = (e1 * aa + e2 * vt) / (e1 * bb + e2)
                ww2 = pp + w
                p2 = jnp.maximum(ww2, kt)
                e1b = jnp.exp(ww2 - p2)
                e2b = jnp.exp(kt - p2)
                return ((e1b * aa + e2b * vt, e1b * bb + e2b, p2), y)
            init = (jnp.zeros((B, C), k.dtype), jnp.zeros((B, C), k.dtype), jnp.full((B, C), NEG_INF, k.dtype))
            _, yT = jax.lax.scan(step, init, (kT, vT))
            return jnp.swapaxes(yT, 0, 1)
        xn = layer_norm(x, ln1_w, ln1_b)
        xx = time_shift(xn)
        xk = xn * tmk + xx * (1 - tmk)
        xv = xn * tmv + xx * (1 - tmv)
        xr = xn * tmr + xx * (1 - tmr)
        k = jnp.einsum('btc,dc->btd', xk, Wk)
        v = jnp.einsum('btc,dc->btd', xv, Wv)
        sr = jax.nn.sigmoid(jnp.einsum('btc,dc->btd', xr, Wr))
        att = wkv(time_decay, time_first, k, v)
        x = x + jnp.einsum('btc,dc->btd', sr * att, Wo)
        xn2 = layer_norm(x, ln2_w, ln2_b)
        xx2 = time_shift(xn2)
        ck = xn2 * cmk + xx2 * (1 - cmk)
        cr = xn2 * cmr + xx2 * (1 - cmr)
        h = jnp.square(jax.nn.relu(jnp.einsum('btc,hc->bth', ck, Wck)))
        kv = jnp.einsum('bth,ch->btc', h, Wcv)
        rkv = jax.nn.sigmoid(jnp.einsum('btc,dc->btd', cr, Wcr)) * kv
        return x + rkv

    def _L0_ffn_ref(x, lut, gate_idx, up_idx, down_idx):
        import jax, jax.numpy as jnp
        import numpy as np
        HIDDEN = 256
        INTER = 688
        LUT_SIZE = 16

        def _ghost_linear(x, idx, lut):
            w = lut[idx]
            return jnp.einsum('bsh,oh->bso', x, w)
        gate = _ghost_linear(x, gate_idx, lut)
        up = _ghost_linear(x, up_idx, lut)
        h = jax.nn.silu(gate) * up
        return _ghost_linear(h, down_idx, lut)
    x = L0_attn_x
    x = x + 0.5 * _L0_ffn_ref(_layernorm(x, axis=-1), L0_ffn_lut, L0_ffn_gate_idx, L0_ffn_up_idx, L0_ffn_down_idx)
    x = x + _L0_attn_ref(_layernorm(x, axis=-1), L0_attn_ln1_w, L0_attn_ln1_b, L0_attn_ln2_w, L0_attn_ln2_b, L0_attn_time_decay, L0_attn_time_first, L0_attn_tmk, L0_attn_tmv, L0_attn_tmr, L0_attn_Wk, L0_attn_Wv, L0_attn_Wr, L0_attn_Wo, L0_attn_cmk, L0_attn_cmr, L0_attn_Wck, L0_attn_Wcv, L0_attn_Wcr)
    x = x + 0.5 * _L0_ffn_ref(_layernorm(x, axis=-1), L0_ffn_lut, L0_ffn_gate_idx, L0_ffn_up_idx, L0_ffn_down_idx)
    return x

_drawn_inputs = setup_inputs


def setup_inputs(seed=0):
    import zlib

    import numpy as np

    out = dict(_drawn_inputs(seed))
    spreads = {'L0_attn_ln1_w': (1.0, 0.2),
     'L0_attn_ln1_b': (0.0, 0.279),
     'L0_attn_ln2_w': (1.0, 0.2),
     'L0_attn_ln2_b': (0.0, 0.1)}
    factors = {}
    for name, (base, spread) in spreads.items():
        noise = np.random.default_rng([zlib.crc32(name.encode()), seed]).standard_normal(out[name].shape)
        drawn = base * np.exp(spread * noise) if base else spread * noise
        out[name] = jnp.asarray(drawn.astype(out[name].dtype))
    for name, factor in factors.items():
        out[name] = (out[name] * factor).astype(out[name].dtype)
    return out
```

```python
from contextlib import ExitStack

import concourse.bass as bass
from concourse import mybir

P = 128
F32 = mybir.dt.float32
F32R = mybir.dt.float32r
I32 = mybir.dt.int32
ALU = mybir.AluOpType
ACT = mybir.ActivationFunctionType

T, C, I, H = 2048, 256, 688, 1024
EPS = 1e-5
NEG_INF = -1e38
CT = 256
NC = T // CT
TT = CT // P
KC = C // P
W = TT * C
IP = 3
KI = 2 * IP
IPAD = KI * P
ILAST = I - (KI - 1) * P
KH = H // P
HP = KH // 2
LUT = 16
PARAMS = ["ln1_w", "ln1_b", "ln2_w", "ln2_b", "time_decay", "time_first", "tmk", "tmv", "tmr", "cmk", "cmr"]
SQUARE = ["Wk", "Wv", "Wr", "Wo", "Wcr"]
LOOP0, LOOP1 = 3, NC


def need(eng, sem, value):
    if isinstance(value, int) and value <= 0:
        return
    eng.wait_ge(sem, value)


def upto(per, index, count):
    if isinstance(count, int) and count <= 0:
        return 0
    return per * (count - 1) + index + 1


def build(nc, x, params, lut, idx_gate, idx_up, idx_down, square, wck, wcv, out):
    with ExitStack() as ctx:
        def sb(name, shape, dt=F32):
            return ctx.enter_context(nc.sbuf_tensor(name, [P, *shape], dt))

        def sem(name):
            return ctx.enter_context(nc.semaphore(name))

        gu = [[ctx.enter_context(nc.psum_tensor(f"gu{i}{j}", [P, 2, CT], F32)) for j in range(2)] for i in range(2)]
        bankA = ctx.enter_context(nc.psum_tensor("bankA", [P, 2, CT], F32))
        bankB = ctx.enter_context(nc.psum_tensor("bankB", [P, 2, CT], F32))
        bankC = ctx.enter_context(nc.psum_tensor("bankC", [P, 2, CT], F32))
        bankT = ctx.enter_context(nc.psum_tensor("bankT", [P, 2, CT], F32))

        w_gate = [sb(f"w_gate{s}", [KC, IPAD], F32R) for s in ("_hi", "_lo")]
        w_up = [sb(f"w_up{s}", [KC, IPAD], F32R) for s in ("_hi", "_lo")]
        w_down = [sb(f"w_down{s}", [KI, C], F32R) for s in ("_hi", "_lo")]
        w_sq = [sb(f"w_sq{s}", [len(SQUARE), KC, C], F32R) for s in ("_hi", "_lo")]
        w_ck = [sb(f"w_ck{s}", [KC, H], F32R) for s in ("_hi", "_lo")]
        w_cv = [sb(f"w_cv{s}", [KH, C], F32R) for s in ("_hi", "_lo")]

        ident = sb("ident", [P])
        par = sb("par", [len(PARAMS), KC])
        lutb = sb("lutb", [LUT])
        lutd = sb("lutd", [LUT // 2])
        wdec = sb("wdec", [KC])
        upw = sb("upw", [KC])
        nupw = sb("nupw", [KC])
        mhalf, eps, minus = sb("mhalf", [TT]), sb("eps", [TT]), sb("minus", [TT])

        x_in = sb("x_in", [TT, C])
        z_tok = sb("z_tok", [TT, C])
        z1_tok = sb("z1_tok", [TT, C])
        z2_tok = sb("z2_tok", [TT, C])
        z0 = [sb(f"z0{s}", [KC, CT], F32R) for s in ("_hi", "_lo")]
        sil = sb("sil", [2, W])
        hval = sb("hval", [2, W])
        hid = [sb(f"hid{s}", [KH, CT], F32R) for s in ("_hi", "_lo")]
        x1 = sb("x1", [TT, C])
        mix = [sb(f"mix{s}", [3, KC, CT], F32R) for s in ("_hi", "_lo")]
        cmix = [sb(f"cmix{s}", [2, KC, CT], F32R) for s in ("_hi", "_lo")]
        att = [sb(f"att{s}", [KC, CT], F32R) for s in ("_hi", "_lo")]
        z3 = [sb(f"z3{s}", [KC, CT], F32R) for s in ("_hi", "_lo")]
        st6 = sb("st6", [4, TT, 6])
        mv = sb("mv", [4, TT, 2])
        veps = sb("veps", [4, TT])
        rstd = sb("rstd", [4, TT])
        nbias = sb("nbias", [4, TT])
        y_scale = [sb("y_rstd", [TT]), sb("y_nbias", [TT])]
        tmp2 = sb("tmp2", [2, TT])

        R_RAW = 2 * KC * I + KI * C + 8 * W
        region = sb("region", [R_RAW + len(SQUARE) * KC * C + KC * H])
        at = [0]

        def take(*shape):
            n = 1
            for s in shape:
                n *= s
            v = region[:, at[0]:at[0] + n]
            at[0] += n
            if len(shape) == 2:
                v = v.rearrange("p (a b) -> p a b", a=shape[0])
            if len(shape) == 3:
                v = v.rearrange("p (a b c) -> p a b c", a=shape[0], b=shape[1])
            return v

        idx_gu = take(2, KC, I).bitcast(I32)
        idx_dn = take(KI, C).bitcast(I32)
        leaves = take(8, W)
        raw_sq = take(len(SQUARE), KC, C)
        raw_ck = take(KC, H)
        raw_cv = raw_ck
        end = at[0]
        at[0] = 0
        xn1 = take(KC, CT + 1)
        xn2 = take(KC, CT + 1)
        dx = take(KC, CT)
        xm = take(2, W)
        state = take(3, KC, CT + 1)
        ng = take(KC, CT)
        ex = take(4, KC, CT)
        er = take(KC, CT)
        kv_m = take(KC, CT)
        n1 = take(KC, CT)
        n2 = take(KC, CT)
        y = take(TT, C)
        x1k = take(TT, C)
        x2 = take(TT, C)
        x12 = take(TT, C)
        th = take(TT, C)
        t3 = take(TT, C)
        x3 = take(TT, C)
        out_sb = take(TT, C)
        assert at[0] <= end
        mask = z_tok[:].rearrange("p a b -> p (a b)").bitcast(I32)
        bit0 = z1_tok[:].rearrange("p a b -> p (a b)").bitcast(I32)

        l_par, l_lut, l_idx, l_dn, l_sq, l_ck, l_cv = (sem(f"l_{n}") for n in ("par", "lut", "idx", "dn", "sq", "ck", "cv"))
        s_x, s_out = sem("s_x"), sem("s_out")
        g_ident, g_clear = sem("g_ident"), sem("g_clear")
        v_init, v_lutd, v_bit, v_mask, v_sel, v_wlo, v_raw = (sem(f"v_{n}") for n in ("init", "lutd", "bit", "mask", "sel", "wlo", "raw"))
        a_leaf, a_whi, a_dec, a_raw = (sem(f"a_{n}") for n in ("leaf", "whi", "dec", "raw"))
        v_st, v_mv = [[sem(f"v_{n}{k}") for k in range(4)] for n in ("st", "mv")]
        g_ve, g_pw, g_rs = [[sem(f"g_{n}{k}") for k in range(4)] for n in ("ve", "pw", "rs")]
        g_s2 = sem("g_s2")
        g_mr = [sem(f"g_mr{k}") for k in range(4)]
        g_chain = sem("g_chain")
        g_y, g_x12, g_x1k = sem("g_y"), sem("g_x12"), sem("g_x1k")
        a_z = [sem(f"a_z{k}") for k in range(4)]
        a_zh = {k: sem(f"a_zh{k}") for k in (0, 3)}
        v_zl = {k: sem(f"v_zl{k}") for k in (0, 3)}
        p_t = [sem(f"p_t{k}") for k in range(4)]
        p_gu, a_sil, v_h, a_hh, g_hl = ([sem(f"{n}{s}") for s in "AC"] for n in ("p_gu", "a_sil", "v_h", "a_hh", "g_hl"))
        p_dn = [sem(f"p_dn{s}") for s in "AC"]
        v_x1, v_out = sem("v_x1"), sem("v_out")
        a_cy1, a_xn1, v_dx1 = sem("a_cy1"), sem("a_xn1"), sem("v_dx1")
        v_xm, a_xmh, v_xml = sem("v_xm"), sem("a_xmh"), sem("v_xml")
        p_k, p_v, p_r = sem("p_k"), sem("p_v"), sem("p_r")
        v_cyw, v_pp, v_ng, a_er, a_re, a_ex = (sem(n) for n in ("v_cyw", "v_pp", "v_ng", "a_er", "a_re", "a_ex"))
        v_m, v_ab, v_n1, v_n2, v_d1, v_n, v_dn, v_de, v_rc, v_at, v_atl = (
            sem(n) for n in ("v_m", "v_ab", "v_n1", "v_n2", "v_d1", "v_n", "v_dn", "v_de", "v_rc", "v_at", "v_atl"))
        a_ath = sem("a_ath")
        p_wo, v_x2 = sem("p_wo"), sem("v_x2")
        a_cy2, a_xn2, v_dx2 = sem("a_cy2"), sem("a_xn2"), sem("v_dx2")
        v_cm, a_cmh, v_cml = sem("v_cm"), sem("a_cmh"), sem("v_cml")
        p_cr, a_th = sem("p_cr"), sem("a_th")
        p_ck, a_rl, v_h2, a_h2h, g_h2l = (sem(n) for n in ("p_ck", "a_rl", "v_h2", "a_h2h", "g_h2l"))
        p_cv, v_t3, v_x3 = sem("p_cv"), sem("v_t3"), sem("v_x3")

        def pcol(name, k):
            return par[:, PARAMS.index(name), k:k + 1]

        def flat(t):
            return t[:].rearrange("p a b -> p (a b)") if len(t.shape) == 3 else t

        def ck_bank(p):
            return gu[p // 2][p % 2]

        TILES = [("A", p) for p in range(IP)] + [("C", p) for p in range(IP)] + [("M", p) for p in range(HP)]
        BANKS = [i % 2 for i in range(2 * IP)] + [p // 2 for p in range(HP)]
        SLOTS = [i % 2 for i in range(len(TILES))]
        LAG = {"A": 0, "M": 1, "C": 2}

        def last_user(slot_of, tile, it):
            i = TILES.index(tile)
            for back, js in ((0, range(i - 1, -1, -1)), (1, range(len(TILES) - 1, -1, -1))):
                for j in js:
                    c = it - back - LAG[TILES[j][0]]
                    there = 0 <= c < NC if isinstance(c, int) else True
                    if slot_of[j] == slot_of[i] and there:
                        return TILES[j], c
            return None

        product_of = {"A": v_h[0], "C": v_h[1], "M": v_h2}
        lo_of = {"A": g_hl[0], "C": g_hl[1], "M": g_h2l}

        def wait_slot(eng, slot_of, tile, it, sem_of):
            before = last_user(slot_of, tile, it)
            if before is not None:
                (stage, p), c = before
                need(eng, sem_of[stage], upto(HP if stage == "M" else IP, p, c + 1))

        slices = []
        for p in range(IP):
            c0, c1 = p * 2 * P, min((p + 1) * 2 * P, I)
            for m, wt in enumerate((w_gate, w_up)):
                slices.append((idx_gu[:, m, :, c0:c1], wt[0][:, :, c0:c1], wt[1][:, :, c0:c1], c1 - c0, l_idx, 32))
        for p in range(IP):
            slices.append((idx_dn[:, 2 * p:2 * p + 2, :], w_down[0][:, 2 * p:2 * p + 2, :],
                           w_down[1][:, 2 * p:2 * p + 2, :], C, l_dn, 32))
        NSL = len(slices)
        raws = [(raw_sq[:, j], w_sq[0][:, j], w_sq[1][:, j], l_sq, 16) for j in range(len(SQUARE))]
        raws += [(raw_ck[:, k], w_ck[0][:, k], w_ck[1][:, k], l_ck, 16) for k in range(KC)]
        raws += [(raw_cv.rearrange("p a b -> p (a b)")[:, k * H:(k + 1) * H],
                  w_cv[0][:, k * 4:(k + 1) * 4].rearrange("p a b -> p (a b)"),
                  w_cv[1][:, k * 4:(k + 1) * 4].rearrange("p a b -> p (a b)"), l_cv, 16) for k in range(KC)]
        NRAW = len(raws)

        block = ctx.enter_context(nc.Block())

        @block.sync
        def _(sp):
            sp.dma_start(idx_gu[:, 0], idx_gate).then_inc(l_idx, 16)
            sp.dma_start(lutb[:], lut).then_inc(l_lut, 16)
            sp.dma_start(par[:], params).then_inc(l_par, 16)
            sp.dma_start(idx_gu[:, 1], idx_up).then_inc(l_idx, 16)

            def load_x(a):
                need(sp, v_x1, a)
                sp.dma_start(x_in[:], x[bass.ds(a * CT, CT), :].rearrange("(t p) c -> p t c", p=P)).then_inc(s_x, 16)

            load_x(0)
            sp.wait_ge(g_clear, 1)
            sp.dma_start(idx_dn[:, 0:KI - 1], idx_down[0:(KI - 1) * P].rearrange("(k p) c -> p k c", p=P)).then_inc(l_dn, 16)
            sp.dma_start(idx_dn[0:ILAST, KI - 1], idx_down[(KI - 1) * P:I]).then_inc(l_dn, 16)
            sp.dma_start(raw_sq, square).then_inc(l_sq, 16)
            sp.dma_start(raw_ck, wck).then_inc(l_ck, 16)
            sp.wait_ge(v_raw, len(SQUARE) + KC)
            sp.dma_start(raw_cv, wcv).then_inc(l_cv, 16)

            def store(d):
                sp.wait_ge(v_out, d + 1)
                sp.dma_start(out[bass.ds(d * CT, CT), :].rearrange("(t p) c -> p t c", p=P), out_sb).then_inc(s_out, 16)

            load_x(1)
            load_x(2)
            store(0)
            with sp.Fori(LOOP0, LOOP1) as it:
                load_x(it)
                store(it - 2)
            store(NC - 2)
            store(NC - 1)
            sp.wait_ge(s_out, 16 * NC)

        @block.tensor
        def _(pe):
            def passes(o, lhs, rhs, first, last):
                for n, (i, j) in enumerate(((0, 0), (0, 1), (1, 0))):
                    mm = pe.matmul(o, lhs[i], rhs[j], start=first and n == 0, stop=last and n == 2,
                                   skip_group_check=True)
                return mm

            def transposes(k, c, src, free_sem, free_count):
                pe.wait_ge(a_z[k], c + 1)
                need(pe, free_sem, free_count)
                for t in range(TT):
                    for f in range(KC):
                        mm = pe.transpose(bankT[:, f, t * P:(t + 1) * P], src[:, t, f * P:(f + 1) * P], ident[:])
                mm.then_inc(p_t[k], 1)

            def kvr(b):
                for j, (bank, done, free_sem) in enumerate(((bankA, p_k, a_th), (bankB, p_v, v_x1), (bankC, p_r, v_out))):
                    pe.wait_ge(a_xmh, upto(3, j, b + 1))
                    pe.wait_ge(v_xml, upto(3, j, b + 1))
                    if j == 0:
                        need(pe, free_sem, b)
                    elif j == 1:
                        pe.wait_ge(free_sem, b + 1)
                    else:
                        need(pe, free_sem, b - 1)
                    for m in range(KC):
                        for k in range(KC):
                            mm = passes(bank[:, m, :], [w[:, j, k, m * P:(m + 1) * P] for w in w_sq],
                                        [h[:, j, k, :] for h in mix], k == 0, k == KC - 1)
                    mm.then_inc(done, 1)

            def cv(d, rs):
                pe.wait_ge(a_er, rs)
                for g in range(HP):
                    pe.wait_ge(a_h2h, upto(HP, g, d + 1))
                    pe.wait_ge(g_h2l, upto(HP, g, d + 1))
                for t in range(TT):
                    for k in range(KH):
                        mm = passes(bankC[:, t, :], [h[:, k, t * P:(t + 1) * P] for h in hid],
                                    [w[:, k, :] for w in w_cv], k == 0, k == KH - 1)
                mm.then_inc(p_cv, 1)

            def gate_up(s, c, p, bank, z):
                for m, w in enumerate((w_gate, w_up)):
                    for i in range(2):
                        col = (2 * p + i) * P
                        for k in range(KC):
                            mm = passes(bank[m][:, i, :], [u[:, k, col:col + P] for u in w],
                                        [h[:, k, :] for h in z], k == 0, k == KC - 1)
                mm.then_inc(p_gu[s], 1)

            def down(s, c, bank):
                for g, pairs in enumerate(((0, 1), (2,))):
                    for p in pairs:
                        pe.wait_ge(a_hh[s], upto(IP, p, c + 1))
                        pe.wait_ge(g_hl[s], upto(IP, p, c + 1))
                    for t in range(TT):
                        for p in pairs:
                            for k in (2 * p, 2 * p + 1):
                                mm = passes(bank[:, t, :], [h[:, k, t * P:(t + 1) * P] for h in hid],
                                            [w[:, k, :] for w in w_down], k == 0 and t == 0, k == KI - 1)
                mm.then_inc(p_dn[s], 1)

            def att_out(b):
                pe.wait_ge(a_ath, b + 1)
                pe.wait_ge(v_atl, b + 1)
                pe.wait_ge(v_ng, b + 1)
                for t in range(TT):
                    for k in range(KC):
                        mm = passes(bankA[:, t, :], [h[:, k, t * P:(t + 1) * P] for h in att],
                                    [w[:, 3, k, :] for w in w_sq], k == 0, k == KC - 1)
                mm.then_inc(p_wo, 1)

            def cr(b):
                pe.wait_ge(a_cmh, upto(2, 1, b + 1))
                pe.wait_ge(v_cml, upto(2, 1, b + 1))
                pe.wait_ge(v_x2, b + 1)
                for t in range(TT):
                    for k in range(KC):
                        mm = passes(bankA[:, t, :], [h[:, 1, k, t * P:(t + 1) * P] for h in cmix],
                                    [w[:, 4, k, :] for w in w_sq], k == 0, k == KC - 1)
                mm.then_inc(p_cr, 1)

            def ck(b, g):
                for i in range(2):
                    col = (2 * g + i) * P
                    for k in range(KC):
                        mm = passes(ck_bank(g)[:, i, :], [u[:, k, col:col + P] for u in w_ck],
                                    [h[:, 0, k, :] for h in cmix], k == 0, k == KC - 1)
                mm.then_inc(p_ck, 1)

            def iteration(it, A, B, D):
                a, b, d = it, it - 1, it - 2
                if B:
                    kvr(b)
                if D:
                    cv(d, b + 1 if B else NC)
                if A:
                    transposes(0, a, z_tok, a_xn1, a)
                    pe.wait_ge(a_zh[0], a + 1)
                    pe.wait_ge(v_zl[0], a + 1)
                    for p in range(IP):
                        wait_slot(pe, BANKS, ("A", p), it, product_of)
                        gate_up(0, a, p, gu[p % 2], z0)
                if D:
                    transposes(3, d, z_tok, *((v_zl[0], a + 1) if A else (a_xn1, NC)))
                    if not A and not B:
                        pe.wait_ge(a_xn2, NC)
                if A:
                    if B:
                        pe.wait_ge(v_n2, b + 1)
                    down(0, a, bankB)
                if D:
                    pe.wait_ge(a_zh[3], d + 1)
                    pe.wait_ge(v_zl[3], d + 1)
                    for p in range(IP):
                        wait_slot(pe, BANKS, ("C", p), it, product_of)
                        gate_up(1, d, p, gu[(p + 1) % 2], z3)
                if B:
                    att_out(b)
                if D:
                    pe.wait_ge(v_t3, d + 1)
                    down(1, d, bankC)
                if B:
                    transposes(2, b, z2_tok, *((v_zl[3], d + 1) if D else (v_zl[0], a + 1)))
                if A:
                    transposes(1, a, z1_tok, *((a_xn2, b + 1) if B else (v_zl[0], a + 1)))
                if B:
                    cr(b)
                    for g in range(HP):
                        if g % 2 == 0:
                            wait_slot(pe, BANKS, ("M", g), it, product_of)
                        ck(b, g)

            pe.wait_ge(g_ident, 2)
            pe.wait_ge(v_wlo, NSL)
            pe.wait_ge(a_whi, NSL)
            iteration(0, True, False, False)
            pe.wait_ge(v_raw, NRAW)
            iteration(1, True, True, False)
            iteration(2, True, True, True)
            with pe.Fori(LOOP0, LOOP1) as it:
                iteration(it, True, True, True)
            iteration(NC, False, True, True)
            iteration(NC + 1, False, False, True)

        @block.scalar
        def _(act):
            def split_hi(dst, src):
                return act.copy(dst, src)

            def prologue():
                act.wait_ge(v_lutd, 1)
                for n, (_, hi, _, cols, _, _) in enumerate(slices):
                    act.wait_ge(v_bit, n + 1)
                    need(act, v_wlo, n)
                    for j in range(8):
                        ins = act.activation(leaves[:, j, 0:2 * cols], bit0[:, 0:2 * cols], ACT.Identity,
                                             bias=lutb[:, 2 * j:2 * j + 1], scale=lutd[:, j:j + 1])
                    ins.then_inc(a_leaf, 1)
                    act.wait_ge(v_sel, 3 * (n + 1))
                    split_hi(hi, leaves[:, 0, 0:2 * cols].rearrange("p (k c) -> p k c", k=2)).then_inc(a_whi, 1)
                for n, (raw, hi, _, ls, cnt) in enumerate(raws):
                    act.wait_ge(ls, cnt)
                    split_hi(hi, raw).then_inc(a_raw, 1)
                act.wait_ge(l_par, 16)
                act.activation(wdec[:], par[:, PARAMS.index("time_decay"), :], ACT.Exp).then_inc(a_dec, 1)

            def normalise(k, c, dst, src, free):
                act.wait_ge(g_rs[k], c + 1)
                for s, v in free:
                    need(act, s, v)
                for t in range(TT):
                    ins = act.activation(dst[:, t, :], src[:, t, :], ACT.Identity, bias=nbias[:, k, t:t + 1],
                                         scale=rstd[:, k, t:t + 1])
                ins.then_inc(a_z[k], 1)

            def affine(k, c, xn, cy, done, wn, bn, free):
                for s, v in free:
                    need(act, s, v)
                act.copy(xn[:, :, 0:1], xn[:, :, CT:CT + 1]).then_inc(cy, 1)
                act.wait_ge(p_t[k], c + 1)
                act.wait_ge(cy, c + 1)
                for f in range(KC):
                    ins = act.activation(xn[:, f, 1:CT + 1], bankT[:, f, :], ACT.Identity, bias=pcol(bn, f), scale=pcol(wn, f))
                ins.then_inc(done, 1)

            def iteration(it, A, B, D):
                a, b, d = it, it - 1, it - 2
                if A:
                    normalise(0, a, z_tok, x_in, [(p_t[0], a), (p_t[3], d)])
                if B:
                    act.wait_ge(p_r, b + 1)
                    need(act, v_de, b)
                    act.activation(flat(er), flat(bankC), ACT.Exp, scale=-1.0).then_inc(a_er, 1)
                    act.wait_ge(v_ng, b + 1)
                    need(act, v_dn, b)
                    act.activation(ex[:, 0], ng, ACT.Relu, scale=-1.0)
                    act.activation(ex[:, 1], ng, ACT.Relu)
                    for f in range(KC):
                        act.activation(ex[:, 2, f], ng[:, f], ACT.Relu, bias=upw[:, f:f + 1], scale=-1.0)
                        ins = act.activation(ex[:, 3, f], ng[:, f], ACT.Relu, bias=nupw[:, f:f + 1])
                    ins.then_inc(a_re, 1)
                    act.wait_ge(a_re, b + 1)
                    act.activation(ex[:, 0:2], ex[:, 0:2], ACT.Exp, scale=-1.0).then_inc(a_ex, 1)
                    act.activation(ex[:, 2:4], ex[:, 2:4], ACT.Exp, scale=-1.0).then_inc(a_ex, 1)
                if A:
                    act.wait_ge(p_t[0], a + 1)
                    need(act, p_gu[0], upto(IP, IP - 1, a))
                    split_hi(z0[0][:], bankT[:]).then_inc(a_zh[0], 1)
                if D:
                    normalise(3, d, z_tok, x3, [(p_t[0], a + 1) if A else (p_t[3], d)])
                if A:
                    for p in range(IP):
                        ffn_pair(0, a, p, it, [(p_cv, d + 1) if D else (p_dn[0], a)])
                if D:
                    act.wait_ge(p_t[3], d + 1)
                    need(act, p_gu[1], upto(IP, IP - 1, d))
                    split_hi(z3[0][:], bankT[:]).then_inc(a_zh[3], 1)
                if B:
                    act.wait_ge(v_at, b + 1)
                    need(act, p_wo, b)
                    split_hi(att[0][:], n1).then_inc(a_ath, 1)
                if D:
                    for p in range(IP):
                        ffn_pair(1, d, p, it, [(p_dn[0], a + 1) if A else (p_cv, d + 1)])
                if B:
                    normalise(2, b, z2_tok, x2, [(p_t[2], b)])
                if A:
                    normalise(1, a, z1_tok, x1, [(p_t[1], a)])
                if B:
                    affine(2, b, xn2, a_cy2, a_xn2, "ln2_w", "ln2_b", [(v_cm, upto(2, 1, b))])
                    for j in (0, 1):
                        act.wait_ge(v_cm, upto(2, j, b + 1))
                        need(act, (p_ck, p_cr)[j], (HP, 1)[j] * b)
                        split_hi(cmix[0][:, j], xm3(j)).then_inc(a_cmh, 1)
                if A:
                    affine(1, a, xn1, a_cy1, a_xn1, "ln1_w", "ln1_b", [(v_xm, upto(3, 2, a))])
                if B:
                    act.wait_ge(p_cr, b + 1)
                    need(act, v_t3, b)
                    act.activation(th, bankA[:], ACT.Tanh, scale=0.5).then_inc(a_th, 1)
                for g in range(HP):
                    if B:
                        act.wait_ge(p_ck, upto(HP, g, b + 1))
                        wait_slot(act, SLOTS, ("M", g), it, product_of)
                        act.activation(sil[:, g % 2], flat(ck_bank(g)), ACT.Relu).then_inc(a_rl, 1)
                        act.wait_ge(v_h2, upto(HP, g, b + 1))
                        if D:
                            act.wait_ge(p_dn[1], d + 1)
                        elif A:
                            act.wait_ge(p_dn[0], a + 1)
                        split_hi(hid[0][:, 2 * g:2 * g + 2], hval[:, g % 2].rearrange("p (a b) -> p a b", a=2)).then_inc(a_h2h, 1)
                    if A and g < 3:
                        act.wait_ge(v_xm, upto(3, g, a + 1))
                        need(act, (p_k, p_v, p_r)[g], a)
                        split_hi(mix[0][:, g], xm3(g % 2)).then_inc(a_xmh, 1)

            def xm3(j):
                return xm[:, j].rearrange("p (a b) -> p a b", a=2)

            def ffn_pair(s, c, p, it, free):
                tile = ("AC"[s], p)
                q = SLOTS[TILES.index(tile)]
                bank = gu[BANKS[TILES.index(tile)]]
                act.wait_ge(p_gu[s], upto(IP, p, c + 1))
                wait_slot(act, SLOTS, tile, it, product_of)
                act.activation(sil[:, q], flat(bank[0]), ACT.Silu).then_inc(a_sil[s], 1)
                act.wait_ge(v_h[s], upto(IP, p, c + 1))
                for fs, fv in free:
                    need(act, fs, fv)
                split_hi(hid[0][:, 2 * p:2 * p + 2], hval[:, q].rearrange("p (a b) -> p a b", a=2)).then_inc(a_hh[s], 1)

            prologue()
            act.wait_ge(v_init, 4)
            iteration(0, True, False, False)
            iteration(1, True, True, False)
            iteration(2, True, True, True)
            with act.Fori(LOOP0, LOOP1) as it:
                iteration(it, True, True, True)
            iteration(NC, False, True, True)
            iteration(NC + 1, False, False, True)

        @block.vector
        def _(dve):
            def lo(dst, whole, hi):
                return dve.tensor_tensor(dst, whole, hi.bitcast(F32), ALU.subtract)

            def prologue():
                dve.wait_ge(l_lut, 16)
                dve.tensor_tensor(lutd[:], lutb[:, 1:LUT:2], lutb[:, 0:LUT:2], ALU.subtract).then_inc(v_lutd, 1)
                for n, (idx, hi, lo_, cols, ls, cnt) in enumerate(slices):
                    dve.wait_ge(ls, cnt)
                    need(dve, a_leaf, n)
                    v2 = 2 * cols
                    dve.tensor_scalar(bit0[:, 0:v2].rearrange("p (k c) -> p k c", k=2), idx, 1, None,
                                      ALU.bitwise_and).then_inc(v_bit, 1)
                    dve.wait_ge(a_leaf, n + 1)
                    for lev in range(3):
                        m = 3 * n + lev
                        need(dve, v_sel, m)
                        dve.tensor_scalar(mask[:, 0:v2].rearrange("p (k c) -> p k c", k=2), idx, 2 << lev, None,
                                          ALU.bitwise_and).then_inc(v_mask, 1)
                        dve.wait_ge(v_mask, m + 1)
                        st = 1 << lev
                        cnt_ = 4 >> lev
                        dve.copy_predicated(leaves[:, 0:8:2 * st, 0:v2],
                                            mask[:, 0:v2].unsqueeze(1).to_broadcast([P, cnt_, v2]),
                                            leaves[:, st:8:2 * st, 0:v2]).then_inc(v_sel, 1)
                    dve.wait_ge(a_whi, n + 1)
                    lo(lo_, leaves[:, 0, 0:v2].rearrange("p (k c) -> p k c", k=2), hi).then_inc(v_wlo, 1)
                for n, (raw, hi, lo_, ls, cnt) in enumerate(raws):
                    dve.wait_ge(a_raw, n + 1)
                    lo(lo_, raw, hi).then_inc(v_raw, 1)
                dve.memset(xn1[:, :, CT:CT + 1], 0.0)
                dve.memset(xn2[:, :, CT:CT + 1], 0.0)
                dve.memset(state[:, 0, :, CT:CT + 1], NEG_INF)
                dve.memset(state[:, 1:3, :, CT:CT + 1], 0.0).then_inc(v_init, 1)
                dve.wait_ge(a_dec, 1)
                dve.tensor_scalar(wdec[:], wdec[:], -1.0, None, ALU.mult).then_inc(v_init, 1)
                dve.wait_ge(v_init, 2)
                dve.tensor_tensor(upw[:], wdec[:], par[:, PARAMS.index("time_first"), :], ALU.add).then_inc(v_init, 1)
                dve.wait_ge(v_init, 3)
                dve.tensor_scalar(nupw[:], upw[:], -1.0, None, ALU.mult).then_inc(v_init, 1)

            def stats(k, c, src):
                for t in range(TT):
                    ins = dve.bn_stats(st6[:, k, t, :], src[:, t, :])
                ins.then_inc(v_st[k], 1)
                dve.wait_ge(v_init, 4)
                dve.wait_ge(v_st[k], c + 1)
                need(dve, g_rs[k], c)
                for t in range(TT):
                    ins = dve.bn_aggr(mv[:, k, t, :], st6[:, k, t, :])
                ins.then_inc(v_mv[k], 1)

            def ffn_pair(s, c, p, it):
                tile = ("AC"[s], p)
                q = SLOTS[TILES.index(tile)]
                bank = gu[BANKS[TILES.index(tile)]]
                dve.wait_ge(a_sil[s], upto(IP, p, c + 1))
                wait_slot(dve, SLOTS, tile, it, lo_of)
                dve.tensor_tensor(hval[:, q], sil[:, q], flat(bank[1]), ALU.mult).then_inc(v_h[s], 1)

            def wkv_state(b):
                dve.tensor_copy(state[:, :, :, 0:1], state[:, :, :, CT:CT + 1]).then_inc(v_cyw, 1)
                dve.wait_ge(v_cyw, b + 1)
                dve.wait_ge(p_k, b + 1)
                for f in range(KC):
                    ins = dve.tensor_tensor_scan(state[:, 0, f, 1:CT + 1], wdec[:, f:f + 1].to_broadcast([P, CT]), bankA[:, f, :],
                                                 state[:, 0, f, 0:1], ALU.add, ALU.max)
                ins.then_inc(v_pp, 1)
                dve.wait_ge(v_pp, b + 1)
                need(dve, a_re, b)
                for f in range(KC):
                    ins = dve.scalar_tensor_tensor(ng[:, f], state[:, 0, f, 0:CT], wdec[:, f:f + 1], bankA[:, f, :],
                                                   ALU.add, ALU.subtract)
                ins.then_inc(v_ng, 1)

            def wkv_scans(b):
                dve.wait_ge(a_ex, 2 * b + 1)
                dve.wait_ge(p_v, b + 1)
                need(dve, v_at, b)
                dve.tensor_tensor(kv_m, ex[:, 1], bankB[:], ALU.mult).then_inc(v_m, 1)
                dve.wait_ge(v_m, b + 1)
                for f in range(KC):
                    for j, add in ((1, kv_m[:, f]), (2, ex[:, 1, f])):
                        ins = dve.tensor_tensor_scan(state[:, j, f, 1:CT + 1], ex[:, 0, f], add, state[:, j, f, 0:1],
                                                     ALU.mult, ALU.add)
                ins.then_inc(v_ab, 1)
                dve.wait_ge(a_ex, 2 * b + 2)
                need(dve, v_atl, b)
                need(dve, a_ath, b)
                dve.tensor_tensor(n2, ex[:, 3], bankB[:], ALU.mult).then_inc(v_n2, 1)

            def wkv_sums(b):
                dve.wait_ge(v_ab, b + 1)
                dve.tensor_tensor(n1, ex[:, 2], state[:, 1, :, 0:CT], ALU.mult).then_inc(v_n1, 1)
                dve.tensor_tensor(kv_m, ex[:, 2], state[:, 2, :, 0:CT], ALU.mult).then_inc(v_d1, 1)
                dve.wait_ge(v_d1, b + 1)
                dve.tensor_tensor(n1, n1, n2, ALU.add).then_inc(v_n, 1)
                dve.tensor_tensor(kv_m, kv_m, ex[:, 3], ALU.add).then_inc(v_dn, 1)

            def wkv_ratio(b):
                dve.wait_ge(v_dn, b + 1)
                dve.scalar_tensor_tensor(n2, er, 1.0, kv_m, ALU.add, ALU.mult).then_inc(v_de, 1)
                dve.wait_ge(v_de, b + 1)
                dve.reciprocal(kv_m, n2).then_inc(v_rc, 1)
                dve.wait_ge(v_rc, b + 1)
                dve.tensor_tensor(n1, n1, kv_m, ALU.mult).then_inc(v_at, 1)

            def mixes(src, j, name, slot, free, done):
                for s, v in free:
                    need(dve, s, v)
                for f in range(KC):
                    ins = dve.scalar_tensor_tensor(xm[:, slot, f * CT:(f + 1) * CT], dx[:, f], pcol(name, f), src[:, f, 0:CT],
                                                   ALU.mult, ALU.add)
                ins.then_inc(done, 1)

            def xm3(j):
                return xm[:, j].rearrange("p (a b) -> p a b", a=2)

            def iteration(it, A, B, D):
                a, b, d = it, it - 1, it - 2
                if A:
                    dve.wait_ge(s_x, 16 * (a + 1))
                    stats(0, a, x_in)
                if B:
                    wkv_state(b)
                if D:
                    dve.wait_ge(p_cv, d + 1)
                    need(dve, v_x3, d)
                    dve.scalar_tensor_tensor(t3, th, 1.0, bankC[:], ALU.add, ALU.mult).then_inc(v_t3, 1)
                    dve.wait_ge(v_t3, d + 1)
                    dve.wait_ge(g_x12, d + 1)
                    need(dve, v_out, d)
                    dve.scalar_tensor_tensor(x3, t3, 0.5, x12, ALU.mult, ALU.add).then_inc(v_x3, 1)
                    dve.wait_ge(v_x3, d + 1)
                    stats(3, d, x3)
                if A:
                    dve.wait_ge(a_zh[0], a + 1)
                    lo(z0[1][:], bankT[:], z0[0][:]).then_inc(v_zl[0], 1)
                if B:
                    wkv_scans(b)
                if A:
                    ffn_pair(0, a, 0, it)
                if B:
                    wkv_sums(b)
                if A:
                    ffn_pair(0, a, 1, it)
                    ffn_pair(0, a, 2, it)
                if D:
                    dve.wait_ge(a_zh[3], d + 1)
                    lo(z3[1][:], bankT[:], z3[0][:]).then_inc(v_zl[3], 1)
                if B:
                    wkv_ratio(b)
                    dve.wait_ge(a_ath, b + 1)
                    lo(att[1][:], n1, att[0][:]).then_inc(v_atl, 1)
                if A:
                    dve.wait_ge(p_dn[0], a + 1)
                    need(dve, g_x1k, a)
                    need(dve, a_z[1], a)
                    dve.scalar_tensor_tensor(x1[:], bankB[:], 0.5, x_in[:], ALU.mult, ALU.add).then_inc(v_x1, 1)
                    dve.wait_ge(v_x1, a + 1)
                    stats(1, a, x1)
                if D:
                    for p in range(IP):
                        ffn_pair(1, d, p, it)
                if B:
                    dve.wait_ge(p_wo, b + 1)
                    dve.wait_ge(g_y, b + 1)
                    need(dve, g_x12, b)
                    dve.tensor_tensor(x2, bankA[:], y, ALU.add).then_inc(v_x2, 1)
                    dve.wait_ge(v_x2, b + 1)
                    stats(2, b, x2)
                if D:
                    dve.wait_ge(p_dn[1], d + 1)
                    need(dve, s_out, 16 * d)
                    dve.scalar_tensor_tensor(out_sb, bankC[:], 0.5, x3, ALU.mult, ALU.add).then_inc(v_out, 1)
                if B:
                    dve.wait_ge(a_xn2, b + 1)
                    need(dve, v_xm, upto(3, 2, b + 1))
                    dve.tensor_tensor(dx, xn2[:, :, 1:CT + 1], xn2[:, :, 0:CT], ALU.subtract).then_inc(v_dx2, 1)
                    dve.wait_ge(v_dx2, b + 1)
                    mixes(xn2, 0, "cmk", 0, [(v_xml, upto(3, 2, b + 1)), (a_xmh, upto(3, 2, b + 1))], v_cm)
                    mixes(xn2, 1, "cmr", 1, [(v_xml, upto(3, 1, b + 1)), (a_xmh, upto(3, 1, b + 1))], v_cm)
                    for j in (0, 1):
                        dve.wait_ge(v_cm, upto(2, j, b + 1))
                        dve.wait_ge(a_cmh, upto(2, j, b + 1))
                        lo(cmix[1][:, j], xm3(j), cmix[0][:, j]).then_inc(v_cml, 1)
                if A:
                    dve.wait_ge(a_xn1, a + 1)
                    need(dve, v_cm, upto(2, 1, b + 1))
                    dve.tensor_tensor(dx, xn1[:, :, 1:CT + 1], xn1[:, :, 0:CT], ALU.subtract).then_inc(v_dx1, 1)
                    dve.wait_ge(v_dx1, a + 1)
                for g in range(HP):
                    if A and g < 3:
                        free = [(v_cml, upto(2, g, b + 1)), (a_cmh, upto(2, g, b + 1))] if g < 2 else [(v_xml, upto(3, 0, a + 1)), (a_xmh, upto(3, 0, a + 1))]
                        mixes(xn1, g, ("tmk", "tmv", "tmr")[g], g % 2, free, v_xm)
                    if B:
                        dve.wait_ge(a_rl, upto(HP, g, b + 1))
                        wait_slot(dve, SLOTS, ("M", g), it, lo_of)
                        dve.tensor_tensor(hval[:, g % 2], sil[:, g % 2], flat(ck_bank(g)), ALU.mult).then_inc(v_h2, 1)
                    if A and g < 3:
                        dve.wait_ge(v_xm, upto(3, g, a + 1))
                        dve.wait_ge(a_xmh, upto(3, g, a + 1))
                        lo(mix[1][:, g], xm3(g % 2), mix[0][:, g]).then_inc(v_xml, 1)

            prologue()
            iteration(0, True, False, False)
            iteration(1, True, True, False)
            iteration(2, True, True, True)
            with dve.Fori(LOOP0, LOOP1) as it:
                iteration(it, True, True, True)
            iteration(NC, False, True, True)
            iteration(NC + 1, False, False, True)

        @block.gpsimd
        def _(pool):
            def rsqrt(k, c):
                pool.wait_ge(v_mv[k], c + 1)
                need(pool, a_z[k], c)
                pool.tensor_tensor(veps[:, k], mv[:, k, :, 1], eps[:], ALU.add).then_inc(g_ve[k], 1)
                pool.wait_ge(g_ve[k], c + 1)
                scale, shift = (rstd[:, k], nbias[:, k]) if k != 1 else (y_scale[0][:], y_scale[1][:])
                if k == 1:
                    need(pool, g_y, c)
                pool.tensor_tensor(scale, veps[:, k], mhalf[:], ALU.pow).then_inc(g_pw[k], 1)
                pool.wait_ge(g_pw[k], c + 1)
                pool.tensor_tensor(veps[:, k], mv[:, k, :, 0], scale, ALU.mult).then_inc(g_mr[k], 1)
                pool.wait_ge(g_mr[k], c + 1)
                pool.tensor_tensor(shift, veps[:, k], minus[:], ALU.mult).then_inc(g_rs[k] if k != 1 else g_chain, 1)

            def second_norm(c):
                s1 = y_scale[0][:]
                n = 5 * c
                pool.wait_ge(g_chain, n + 1)
                pool.tensor_tensor(tmp2[:, 0], s1, s1, ALU.mult).then_inc(g_chain, 1)
                pool.wait_ge(g_chain, n + 2)
                pool.tensor_tensor(tmp2[:, 1], tmp2[:, 0], mv[:, 1, :, 1], ALU.mult).then_inc(g_chain, 1)
                pool.wait_ge(g_chain, n + 3)
                pool.tensor_tensor(tmp2[:, 0], tmp2[:, 1], eps[:], ALU.add).then_inc(g_chain, 1)
                pool.wait_ge(g_chain, n + 4)
                pool.tensor_tensor(tmp2[:, 1], tmp2[:, 0], mhalf[:], ALU.pow).then_inc(g_chain, 1)
                pool.wait_ge(g_chain, n + 5)
                pool.tensor_tensor(rstd[:, 1], tmp2[:, 1], s1, ALU.mult).then_inc(g_s2, 1)
                pool.tensor_tensor(nbias[:, 1], tmp2[:, 1], y_scale[1][:], ALU.mult).then_inc(g_rs[1], 1)

            def lo_pair(tile, c, hi_sem, done):
                p = tile[1]
                pool.wait_ge(hi_sem, upto(HP if tile[0] == "M" else IP, p, c + 1))
                whole = hval[:, SLOTS[TILES.index(tile)]].rearrange("p (a b) -> p a b", a=2)
                pool.tensor_tensor(hid[1][:, 2 * p:2 * p + 2], whole, hid[0][:, 2 * p:2 * p + 2].bitcast(F32),
                                   ALU.subtract).then_inc(done, 1)

            def iteration(it, A, B, D):
                a, b, d = it, it - 1, it - 2
                if A:
                    rsqrt(0, a)
                if D:
                    rsqrt(3, d)
                if A:
                    for p in range(IP):
                        lo_pair(("A", p), a, a_hh[0], g_hl[0])
                    rsqrt(1, a)
                    second_norm(a)
                if D:
                    for p in range(IP):
                        lo_pair(("C", p), d, a_hh[1], g_hl[1])
                if B:
                    rsqrt(2, b)
                    need(pool, v_x3, b)
                    pool.tensor_tensor(x12, x2, x1k, ALU.add).then_inc(g_x12, 1)
                if A:
                    x12_done = b + 1 if isinstance(it, int) else pool.snap(b + 1)
                    pool.wait_ge(v_init, 4)
                    need(pool, g_x12, x12_done)
                    pool.tensor_scalar(x1k, x1[:], 1.0, 0.0, ALU.mult, ALU.add).then_inc(g_x1k, 1)
                    pool.wait_ge(v_init, 4)
                    need(pool, v_x2, x12_done)
                    for t in range(TT):
                        ins = pool.tensor_scalar(y[:, t], x1[:, t], y_scale[0][:, t:t + 1], y_scale[1][:, t:t + 1],
                                                 ALU.mult, ALU.add)
                    ins.then_inc(g_y, 1)
                if B:
                    for g in range(HP):
                        lo_pair(("M", g), b, a_h2h, g_h2l)

            idx_last = idx_dn[:, KI - 1, :]
            pool.memset(idx_last, 0).then_inc(g_clear, 1)
            for const, value in ((mhalf, -0.5), (eps, EPS), (minus, -1.0)):
                pool.memset(const[:], value)
            for w in (*w_gate, *w_up):
                ins = pool.memset(w[:, :, I:IPAD].bitcast(F32), 0.0)
            pool.memset(ident[:], 0.0).then_inc(g_ident, 1)
            pool.wait_ge(g_ident, 1)
            pool.affine_select(out=ident[:], in_=ident[:], compare_op=ALU.not_equal, fill=1.0, base=0,
                               pattern=[[-1, P]], channel_multiplier=1).then_inc(g_ident, 1)
            pool.wait_ge(v_init, 4)
            iteration(0, True, False, False)
            iteration(1, True, True, False)
            iteration(2, True, True, True)
            with pool.Fori(LOOP0, LOOP1) as it:
                iteration(it, True, True, True)
            iteration(NC, False, True, True)
            iteration(NC + 1, False, False, True)

        return nc


def kernel(**inputs):
    import numpy as np
    import concourse.bacc as bacc
    from concourse.bass_utils import run_bass_kernel_spmd

    def tiles(w):
        r, c = w.shape
        return np.ascontiguousarray(w.reshape(r // P, P, c).transpose(1, 0, 2))

    def get(name):
        return np.asarray(inputs["L0_" + name])

    params = np.stack([get("attn_" + n) for n in PARAMS]).reshape(len(PARAMS), KC, P).transpose(2, 0, 1)
    arrays = {
        "in_x": get("attn_x").reshape(T, C),
        "in_params": np.ascontiguousarray(params),
        "in_lut": np.ascontiguousarray(np.broadcast_to(get("ffn_lut"), (P, LUT))),
        "in_gate": tiles(get("ffn_gate_idx").T),
        "in_up": tiles(get("ffn_up_idx").T),
        "in_down": np.ascontiguousarray(get("ffn_down_idx").T),
        "in_square": np.ascontiguousarray(np.stack([tiles(get("attn_" + n).T) for n in SQUARE], axis=1)),
        "in_wck": tiles(get("attn_Wck").T),
        "in_wcv": tiles(get("attn_Wcv").T),
    }
    nc = bacc.Bacc("TRN2", target_bir_lowering=False, num_devices=1)
    args = [nc.dram_tensor(n, a.shape, mybir.dt.from_np(a.dtype), kind="ExternalInput").ap() for n, a in arrays.items()]
    out = nc.dram_tensor("out", (T, C), F32, kind="ExternalOutput").ap()
    build(nc, *args, out)
    r = run_bass_kernel_spmd(nc, [arrays], core_ids=[0])
    return r.results[0]["out"].reshape(1, T, C)
```

```python
from contextlib import ExitStack

import concourse.bass as bass
from concourse import mybir

P = 128
F32 = mybir.dt.float32
F32R = mybir.dt.float32r
I32 = mybir.dt.int32
ALU = mybir.AluOpType
ACT = mybir.ActivationFunctionType

T, C, I, H = 2048, 256, 688, 1024
EPS = 1e-5
NEG_INF = -1e38
CT = 256
NC = T // CT
TT = CT // P
KC = C // P
W = TT * C
IP = 3
KI = 2 * IP
IPAD = KI * P
ILAST = I - (KI - 1) * P
KH = H // P
HP = KH // 2
HID = KH + 2
LUT = 16
PARAMS = ["ln1_w", "ln1_b", "ln2_w", "ln2_b", "time_decay", "time_first", "tmk", "tmv", "tmr", "cmk", "cmr"]
SQUARE = ["Wk", "Wv", "Wr", "Wo", "Wcr"]
LOOP0, LOOP1 = 4, NC


def need(eng, sem, value):
    if isinstance(value, int) and value <= 0:
        return
    eng.wait_ge(sem, value)


def upto(per, index, count):
    if isinstance(count, int) and count <= 0:
        return 0
    return per * (count - 1) + index + 1


def build(nc, x, params, lut, idx_gate, idx_up, idx_down, square, wck, wcv, out):
    with ExitStack() as ctx:
        def sb(name, shape, dt=F32):
            return ctx.enter_context(nc.sbuf_tensor(name, [P, *shape], dt))

        def sem(name):
            return ctx.enter_context(nc.semaphore(name))

        gu = [[ctx.enter_context(nc.psum_tensor(f"gu{i}{j}", [P, 2, CT], F32)) for j in range(2)] for i in range(2)]
        bankA = ctx.enter_context(nc.psum_tensor("bankA", [P, 2, CT], F32))
        bankB = ctx.enter_context(nc.psum_tensor("bankB", [P, 2, CT], F32))
        bankC = ctx.enter_context(nc.psum_tensor("bankC", [P, 2, CT], F32))
        bankT = ctx.enter_context(nc.psum_tensor("bankT", [P, 2, CT], F32))

        w_gate = [sb(f"w_gate{s}", [KC, IPAD], F32R) for s in ("_hi", "_lo")]
        w_up = [sb(f"w_up{s}", [KC, IPAD], F32R) for s in ("_hi", "_lo")]
        w_down = [sb(f"w_down{s}", [KI, C], F32R) for s in ("_hi", "_lo")]
        w_sq = [sb(f"w_sq{s}", [len(SQUARE), KC, C], F32R) for s in ("_hi", "_lo")]
        w_ck = [sb(f"w_ck{s}", [KC, H], F32R) for s in ("_hi", "_lo")]
        w_cv = [sb(f"w_cv{s}", [KH, C], F32R) for s in ("_hi", "_lo")]

        ident = sb("ident", [P])
        par = sb("par", [len(PARAMS), KC])
        lutb = sb("lutb", [LUT])
        lutd = sb("lutd", [LUT // 2])
        wdec = sb("wdec", [KC])
        upw = sb("upw", [KC])
        nupw = sb("nupw", [KC])
        mhalf, eps, minus = sb("mhalf", [TT]), sb("eps", [TT]), sb("minus", [TT])

        x_in = sb("x_in", [TT, C])
        z03_tok = sb("z03_tok", [TT, C])
        z12_tok = sb("z12_tok", [TT, C])
        z0 = [sb(f"z0{s}", [KC, CT], F32R) for s in ("_hi", "_lo")]
        sil = sb("sil", [2, W])
        hval = sb("hval", [2, W])
        hid = [sb(f"hid{s}", [HID, CT], F32R) for s in ("_hi", "_lo")]
        x1 = sb("x1", [TT, C])
        EARLY = len(SQUARE) * W + KC * H + KH * C + W
        with nc.sbuf_tensor("early", [P, EARLY], F32) as early:
            pass
        mix = [sb(f"mix{s}", [3, KC, CT], F32R) for s in ("_hi", "_lo")]
        cmix = [sb(f"cmix{s}", [2, KC, CT], F32R) for s in ("_hi", "_lo")]
        att = [sb(f"att{s}", [KC, CT], F32R) for s in ("_hi", "_lo")]
        z3 = [sb(f"z3{s}", [KC, CT], F32R) for s in ("_hi", "_lo")]
        st6 = sb("st6", [4, TT, 6])
        mv = sb("mv", [4, TT, 2])
        veps = sb("veps", [4, TT])
        rstd = sb("rstd", [4, TT])
        nbias = sb("nbias", [4, TT])
        y_scale = [sb("y_rstd", [TT]), sb("y_nbias", [TT])]
        tmp2 = sb("tmp2", [2, TT])

        DECODE = 2 * KC * I + KI * C + 2 * 8 * W
        region = sb("region", [DECODE])
        at = [0]

        def take(*shape):
            n = 1
            for s in shape:
                n *= s
            v = region[:, at[0]:at[0] + n]
            at[0] += n
            if len(shape) == 2:
                v = v.rearrange("p (a b) -> p a b", a=shape[0])
            if len(shape) == 3:
                v = v.rearrange("p (a b c) -> p a b c", a=shape[0], b=shape[1])
            return v

        idx_gu = take(2, KC, I).bitcast(I32)
        idx_dn = take(KI, C).bitcast(I32)
        leaves = [take(8, W), take(8, W)]
        bit0 = [z12_tok[:].rearrange("p a b -> p (a b)").bitcast(I32), early[:, EARLY - W:EARLY].bitcast(I32)]
        mask = x1[:].rearrange("p a b -> p (a b)").bitcast(I32)
        end = at[0]
        at[0] = 0
        xn1 = take(KC, CT + 1)
        xn2 = take(KC, CT + 1)
        dx = take(KC, CT)
        xm = take(2, W)
        state = take(3, KC, CT + 1)
        ng = take(KC, CT)
        ex = take(4, KC, CT)
        er = take(KC, CT)
        kv_m = take(KC, CT)
        n1 = take(KC, CT)
        n2 = take(KC, CT)
        y = take(TT, C)
        x1k = take(TT, C)
        x2 = take(TT, C)
        x12 = take(TT, C)
        th = take(TT, C)
        x3 = take(TT, C)
        out_sb = take(TT, C)
        assert at[0] <= end
        raw_sq = [early[:, j * W:(j + 1) * W].rearrange("p (a b) -> p a b", a=KC) for j in range(len(SQUARE))]
        at_ck, at_cv = len(SQUARE) * W, len(SQUARE) * W + KC * H
        raw_ck = [early[:, at_ck + k * H:at_ck + (k + 1) * H] for k in range(KC)]
        raw_cv = [early[:, at_cv + k * W:at_cv + (k + 1) * W].rearrange("p (a b) -> p a b", a=2) for k in range(KH // 2)]

        l_par, l_lut, l_dn, l_raw = (sem(f"l_{n}") for n in ("par", "lut", "dn", "raw"))
        l_idx = [sem(f"l_idx{p}") for p in range(IP)]
        s_x, s_out = sem("s_x"), sem("s_out")
        g_ident, g_clear, g_leaf, g_wlo = (sem(f"g_{n}") for n in ("ident", "clear", "leaf", "wlo"))
        v_init, v_clear, v_lutd, v_bit, v_mask, v_sel, v_raw = (sem(f"v_{n}") for n in ("init", "clear", "lutd", "bit", "mask", "sel", "raw"))
        a_leaf, a_whi, a_dec, a_raw = (sem(f"a_{n}") for n in ("leaf", "whi", "dec", "raw"))
        v_st, v_mv = [[sem(f"v_{n}{k}") for k in range(4)] for n in ("st", "mv")]
        g_ve, g_pw, g_rs = [[sem(f"g_{n}{k}") for k in range(4)] for n in ("ve", "pw", "rs")]
        g_s2 = sem("g_s2")
        g_mr = [sem(f"g_mr{k}") for k in range(4)]
        g_chain = sem("g_chain")
        g_y, g_x12, g_x1k = sem("g_y"), sem("g_x12"), sem("g_x1k")
        a_z = [sem(f"a_z{k}") for k in range(4)]
        a_zh = {k: sem(f"a_zh{k}") for k in (0, 3)}
        v_zl = {k: sem(f"v_zl{k}") for k in (0, 3)}
        p_t = [sem(f"p_t{k}") for k in range(4)]
        p_gu, a_sil, v_h, a_hh, g_hl = ([sem(f"{n}{s}") for s in "AC"] for n in ("p_gu", "a_sil", "v_h", "a_hh", "g_hl"))
        p_dn = [sem(f"p_dn{s}") for s in "AC"]
        v_x1, v_out = sem("v_x1"), sem("v_out")
        a_cy1, a_xn1, v_dx1 = sem("a_cy1"), sem("a_xn1"), sem("v_dx1")
        v_xm, a_xmh, v_xml = sem("v_xm"), sem("a_xmh"), sem("v_xml")
        p_k, p_v, p_r = sem("p_k"), sem("p_v"), sem("p_r")
        v_cyw, v_pp, v_ng, a_er, a_re, a_ex = (sem(n) for n in ("v_cyw", "v_pp", "v_ng", "a_er", "a_re", "a_ex"))
        v_m, v_ab, v_n1, v_n2, v_d1, v_n, v_dn, v_de, v_rc, v_at, v_atl = (
            sem(n) for n in ("v_m", "v_ab", "v_n1", "v_n2", "v_d1", "v_n", "v_dn", "v_de", "v_rc", "v_at", "v_atl"))
        a_ath = sem("a_ath")
        p_wo, v_x2 = sem("p_wo"), sem("v_x2")
        a_cy2, a_xn2, v_dx2 = sem("a_cy2"), sem("a_xn2"), sem("v_dx2")
        v_cm, a_cmh, v_cml = sem("v_cm"), sem("a_cmh"), sem("v_cml")
        p_cr, a_th = sem("p_cr"), sem("a_th")
        p_ck, a_rl, v_h2, a_h2h, g_h2l = (sem(n) for n in ("p_ck", "a_rl", "v_h2", "a_h2h", "g_h2l"))
        p_cv, v_t3, v_x3 = sem("p_cv"), sem("v_t3"), sem("v_x3")

        def pcol(name, k):
            return par[:, PARAMS.index(name), k:k + 1]

        def flat(t):
            return t[:].rearrange("p a b -> p (a b)") if len(t.shape) == 3 else t

        def ck_bank(p):
            return gu[BANKS[TILES.index(("M", p))]][p % 2]

        TILES = [("A", 0), ("M", 0), ("M", 1), ("M", 2), ("M", 3), ("A", 1), ("A", 2), ("C", 0), ("C", 1), ("C", 2)]
        BANKS = [0, 1, 1, 0, 0, 1, 0, 1, 0, 1]
        SLOTS = [i % 2 for i in range(len(TILES))]
        PLACES = [0, 1, 2, 3, 4, 1, 2, 3, 4, 0]
        LAG = {"A": 0, "M": 2, "C": 2}

        def hid_at(stage, k):
            return 2 * PLACES[TILES.index((stage, k // 2))] + k % 2

        def hid_pair(tile):
            q = 2 * PLACES[TILES.index(tile)]
            return slice(q, q + 2)

        def last_user(slot_of, tile, it):
            i = TILES.index(tile)
            for back, js in ((0, range(i - 1, -1, -1)), (1, range(len(TILES) - 1, -1, -1))):
                for j in js:
                    c = it - back - LAG[TILES[j][0]]
                    there = 0 <= c < NC if isinstance(c, int) else True
                    if slot_of[j] == slot_of[i] and there:
                        return TILES[j], c
            return None

        product_of = {"A": v_h[0], "C": v_h[1], "M": v_h2}
        lo_of = {"A": g_hl[0], "C": g_hl[1], "M": g_h2l}

        def wait_slot(eng, slot_of, tile, it, sem_of):
            before = last_user(slot_of, tile, it)
            if before is not None:
                (stage, p), c = before
                need(eng, sem_of[stage], upto(HP if stage == "M" else IP, p, c + 1))

        slices = []
        for p in range(IP):
            c0, c1 = p * 2 * P, min((p + 1) * 2 * P, I)
            for m, wt in enumerate((w_gate, w_up)):
                slices.append((idx_gu[:, m, :, c0:c1], wt[0][:, :, c0:c1], wt[1][:, :, c0:c1], c1 - c0, l_idx[p]))
        for p in range(IP):
            slices.append((idx_dn[:, 2 * p:2 * p + 2, :], w_down[0][:, 2 * p:2 * p + 2, :],
                           w_down[1][:, 2 * p:2 * p + 2, :], C, l_dn))
        NSL, NGU = len(slices), 2 * IP
        ACT_LEAVES = 4
        raws = [(raw_sq[j], w_sq[0][:, j], w_sq[1][:, j]) for j in range(len(SQUARE))]
        raws += [(raw_ck[k], w_ck[0][:, k], w_ck[1][:, k]) for k in range(KC)]
        raws += [(raw_cv[k], w_cv[0][:, 2 * k:2 * k + 2], w_cv[1][:, 2 * k:2 * k + 2]) for k in range(KH // 2)]
        NRAW = len(raws)

        def two(t, cols):
            return t[:, 0:2 * cols].rearrange("p (k c) -> p k c", k=2)

        block = ctx.enter_context(nc.Block())

        @block.sync
        def _(sp):
            sp.dma_start(lutb[:], lut).then_inc(l_lut, 16)
            def load_x(a):
                need(sp, v_x1, a)
                sp.dma_start(x_in[:], x[bass.ds(a * CT, CT), :].rearrange("(t p) c -> p t c", p=P)).then_inc(s_x, 16)

            for p in range(IP):
                c0, c1 = p * 2 * P, min((p + 1) * 2 * P, I)
                for m, idx in enumerate((idx_gate, idx_up)):
                    sp.dma_start(idx_gu[:, m, :, c0:c1], idx[:, :, c0:c1]).then_inc(l_idx[p], 16)
                if p == 0:
                    load_x(0)
                    sp.dma_start(par[:], params).then_inc(l_par, 16)
            sp.wait_ge(g_clear, 1)
            sp.dma_start(idx_dn[:, 0:KI - 1], idx_down[0:(KI - 1) * P].rearrange("(k p) c -> p k c", p=P)).then_inc(l_dn, 16)
            sp.dma_start(idx_dn[0:ILAST, KI - 1], idx_down[(KI - 1) * P:I]).then_inc(l_dn, 16)
            for j in range(len(SQUARE)):
                sp.dma_start(raw_sq[j], square[:, j]).then_inc(l_raw, 16)
            for k in range(KC):
                sp.dma_start(raw_ck[k], wck[:, k]).then_inc(l_raw, 16)
            for k in range(KH // 2):
                sp.dma_start(raw_cv[k], wcv[:, 2 * k:2 * k + 2]).then_inc(l_raw, 16)

            def store(d):
                sp.wait_ge(v_out, d + 1)
                sp.dma_start(out[bass.ds(d * CT, CT), :].rearrange("(t p) c -> p t c", p=P), out_sb).then_inc(s_out, 16)

            for a in range(1, LOOP0):
                load_x(a)
            store(0)
            with sp.Fori(LOOP0, LOOP1) as it:
                load_x(it)
                store(it - 3)
            for d in range(NC - 3, NC):
                store(d)
            sp.wait_ge(s_out, 16 * NC)

        @block.tensor
        def _(pe):
            def passes(o, lhs, rhs, first, last):
                for n, (i, j) in enumerate(((0, 0), (0, 1), (1, 0))):
                    mm = pe.matmul(o, lhs[i], rhs[j], start=first and n == 0, stop=last and n == 2,
                                   skip_group_check=True)
                return mm

            def transposes(k, c, src, free_sem, free_count):
                pe.wait_ge(a_z[k], c + 1)
                need(pe, free_sem, free_count)
                for t in range(TT):
                    for f in range(KC):
                        mm = pe.transpose(bankT[:, f, t * P:(t + 1) * P], src[:, t, f * P:(f + 1) * P], ident[:])
                mm.then_inc(p_t[k], 1)

            def kvr(b):
                for j, (bank, done, free_sem, count) in enumerate((
                        (bankA, p_k, a_th, b),
                        (bankB, p_v, v_x1, b + 1),
                        (bankC, p_r, v_out, b - 1))):
                    pe.wait_ge(a_xmh, upto(3, j, b + 1))
                    pe.wait_ge(v_xml, upto(3, j, b + 1))
                    need(pe, free_sem, count)
                    for m in range(KC):
                        for k in range(KC):
                            mm = passes(bank[:, m, :], [w[:, j, k, m * P:(m + 1) * P] for w in w_sq],
                                        [h[:, j, k, :] for h in mix], k == 0, k == KC - 1)
                    mm.then_inc(done, 1)

            def cv(c, free_sem, count):
                pe.wait_ge(free_sem, count)
                for k in range(KH):
                    if k % 2 == 0:
                        pe.wait_ge(a_h2h, upto(HP, k // 2, c + 1))
                        pe.wait_ge(g_h2l, upto(HP, k // 2, c + 1))
                    for t in range(TT):
                        mm = passes(bankA[:, t, :], [h[:, hid_at("M", k), t * P:(t + 1) * P] for h in hid],
                                    [w[:, k, :] for w in w_cv], k == 0 and t == 0, k == KH - 1)
                mm.then_inc(p_cv, 1)

            def gate_up(tile, c, it):
                s, p = "AC".index(tile[0]), tile[1]
                bank, z = gu[BANKS[TILES.index(tile)]], (z0, z3)[s]
                wait_slot(pe, BANKS, tile, it, product_of)
                for m, w in enumerate((w_gate, w_up)):
                    for i in range(2):
                        col = (2 * p + i) * P
                        for k in range(KC):
                            mm = passes(bank[m][:, i, :], [u[:, k, col:col + P] for u in w],
                                        [h[:, k, :] for h in z], k == 0, k == KC - 1)
                mm.then_inc(p_gu[s], 1)

            def down(s, c, bank, pairs):
                for p in pairs:
                    pe.wait_ge(a_hh[s], upto(IP, p, c + 1))
                    pe.wait_ge(g_hl[s], upto(IP, p, c + 1))
                    for k in (2 * p, 2 * p + 1):
                        for t in range(TT):
                            mm = passes(bank[:, t, :], [h[:, hid_at("AC"[s], k), t * P:(t + 1) * P] for h in hid],
                                        [w[:, k, :] for w in w_down], k == 0 and t == 0, k == KI - 1)
                if pairs[-1] == IP - 1:
                    mm.then_inc(p_dn[s], 1)

            def att_out(b, free_sem, count):
                pe.wait_ge(a_ath, b + 1)
                pe.wait_ge(v_atl, b + 1)
                pe.wait_ge(free_sem, count)
                for t in range(TT):
                    for k in range(KC):
                        mm = passes(bankA[:, t, :], [h[:, k, t * P:(t + 1) * P] for h in att],
                                    [w[:, 3, k, :] for w in w_sq], k == 0, k == KC - 1)
                mm.then_inc(p_wo, 1)

            def cr(c):
                pe.wait_ge(a_cmh, upto(2, 0, c + 1))
                pe.wait_ge(v_cml, upto(2, 0, c + 1))
                pe.wait_ge(v_x2, c + 1)
                for t in range(TT):
                    for k in range(KC):
                        mm = passes(bankA[:, t, :], [h[:, 0, k, t * P:(t + 1) * P] for h in cmix],
                                    [w[:, 4, k, :] for w in w_sq], k == 0, k == KC - 1)
                mm.then_inc(p_cr, 1)

            def ck(c, g, it):
                if g == 0:
                    pe.wait_ge(a_cmh, upto(2, 1, c + 1))
                    pe.wait_ge(v_cml, upto(2, 1, c + 1))
                if g % 2 == 0:
                    wait_slot(pe, BANKS, ("M", g), it, product_of)
                for i in range(2):
                    col = (2 * g + i) * P
                    for k in range(KC):
                        mm = passes(ck_bank(g)[:, i, :], [u[:, k, col:col + P] for u in w_ck],
                                    [h[:, 1, k, :] for h in cmix], k == 0, k == KC - 1)
                mm.then_inc(p_ck, 1)

            def iteration(it, A, B, C_, D):
                a, b, c, d = it, it - 1, it - 2, it - 3
                if D:
                    pe.wait_ge(a_er, c + 1 if C_ else NC)
                    down(1, d, bankC, (0, 1))
                if B:
                    transposes(1, b, z12_tok, *((a_xn2, c + 1) if C_ else (a_xn2, 0)))
                if D:
                    down(1, d, bankC, (2,))
                if A:
                    transposes(0, a, z03_tok, a_xn1, b + 1)
                if C_:
                    cr(c)
                if A:
                    if A and not B:
                        pe.wait_ge(a_whi, 2)
                        pe.wait_ge(g_wlo, 2)
                    pe.wait_ge(a_zh[0], a + 1)
                    pe.wait_ge(v_zl[0], a + 1)
                    gate_up(("A", 0), a, it)
                if C_:
                    for g in range(HP):
                        ck(c, g, it)
                if B:
                    if B and not C_:
                        pe.wait_ge(v_raw, NRAW)
                    kvr(b)
                if C_:
                    cv(c, *((v_ng, b + 1) if B else (a_th, c + 1)))
                if A:
                    for p in (1, 2):
                        if A and not B:
                            pe.wait_ge(a_whi, 2 * p + 2)
                            pe.wait_ge(g_wlo, 2 * p + 2)
                        gate_up(("A", p), a, it)
                if C_:
                    transposes(3, c, z03_tok, *((v_zl[0], a + 1) if A else (a_xn1, NC) if B else (a_xn2, NC)))
                if A:
                    if B:
                        pe.wait_ge(v_n2, b + 1)
                    else:
                        pe.wait_ge(a_whi, NSL)
                        pe.wait_ge(g_wlo, NSL)
                    down(0, a, bankB, (0, 1))
                if C_:
                    pe.wait_ge(a_zh[3], c + 1)
                    pe.wait_ge(v_zl[3], c + 1)
                    gate_up(("C", 0), c, it)
                if A:
                    down(0, a, bankB, (2,))
                if B:
                    att_out(b, *((v_t3, c + 1) if C_ else (v_ng, b + 1)))
                if C_:
                    gate_up(("C", 1), c, it)
                    gate_up(("C", 2), c, it)
                if B:
                    transposes(2, b, z12_tok, *((v_zl[3], c + 1) if C_ else (v_zl[0], a + 1)))

            pe.wait_ge(g_ident, 2)
            iteration(0, True, False, False, False)
            iteration(1, True, True, False, False)
            iteration(2, True, True, True, False)
            iteration(3, True, True, True, True)
            with pe.Fori(LOOP0, LOOP1) as it:
                iteration(it, True, True, True, True)
            iteration(NC, False, True, True, True)
            iteration(NC + 1, False, False, True, True)
            iteration(NC + 2, False, False, False, True)

        @block.scalar
        def _(act):
            def split_hi(dst, src):
                return act.copy(dst, src)

            def decode(n0, n1):
                def hi_of(n):
                    act.wait_ge(v_sel, 3 * (n + 1))
                    split_hi(slices[n][1], two(leaves[n % 2][:, 0], slices[n][3])).then_inc(a_whi, 1)

                for n in range(n0, n1):
                    cols = slices[n][3]
                    act.wait_ge(v_bit, n + 1)
                    need(act, g_wlo, n - 1)
                    for j in range(ACT_LEAVES):
                        ins = act.activation(leaves[n % 2][:, j, 0:2 * cols], bit0[n % 2][:, 0:2 * cols], ACT.Identity,
                                             bias=lutb[:, 2 * j:2 * j + 1], scale=lutd[:, j:j + 1])
                    ins.then_inc(a_leaf, 1)
                    if n > n0:
                        hi_of(n - 1)
                hi_of(n1 - 1)

            def split_raws():
                act.wait_ge(l_raw, 16 * NRAW)
                for raw, hi, _ in raws:
                    split_hi(hi, raw).then_inc(a_raw, 1)

            def normalise(k, c, dst, src, free):
                act.wait_ge(g_rs[k], c + 1)
                for s, v in free:
                    need(act, s, v)
                for t in range(TT):
                    ins = act.activation(dst[:, t, :], src[:, t, :], ACT.Identity, bias=nbias[:, k, t:t + 1],
                                         scale=rstd[:, k, t:t + 1])
                ins.then_inc(a_z[k], 1)

            def affine(k, c, xn, cy, done, wn, bn, free):
                for s, v in free:
                    need(act, s, v)
                act.copy(xn[:, :, 0:1], xn[:, :, CT:CT + 1]).then_inc(cy, 1)
                act.wait_ge(p_t[k], c + 1)
                act.wait_ge(cy, c + 1)
                for f in range(KC):
                    ins = act.activation(xn[:, f, 1:CT + 1], bankT[:, f, :], ACT.Identity, bias=pcol(bn, f), scale=pcol(wn, f))
                ins.then_inc(done, 1)

            def iteration(it, A, B, C_, D):
                a, b, c, d = it, it - 1, it - 2, it - 3
                if C_:
                    affine(2, c, xn2, a_cy2, a_xn2, "ln2_w", "ln2_b", [(v_cm, upto(2, 1, c))])
                if D:
                    hidden_hi(("C", 2), d, [(p_dn[0], b + 1 if B else NC)])
                if B:
                    normalise(1, b, z12_tok, x1, [(p_t[2], c + 1)])
                if C_:
                    mix_hi(cmix, c, 0, 2, v_cm, a_cmh, p_cr, c)
                if A:
                    normalise(0, a, z03_tok, x_in, [(p_t[3], d + 1)])
                if B:
                    affine(1, b, xn1, a_cy1, a_xn1, "ln1_w", "ln1_b", [(v_xm, upto(3, 2, b))])
                if C_:
                    mix_hi(cmix, c, 1, 2, v_cm, a_cmh, p_ck, HP * c)
                if A:
                    act.wait_ge(p_t[0], a + 1)
                    need(act, p_gu[0], upto(IP, IP - 1, a))
                    split_hi(z0[0][:], bankT[:]).then_inc(a_zh[0], 1)
                if C_:
                    act.wait_ge(p_cr, c + 1)
                    need(act, v_x3, c)
                    act.activation(th, bankA[:], ACT.Tanh, scale=0.5).then_inc(a_th, 1)
                if A and not B:
                    decode(0, NGU)
                if B:
                    mix_hi(mix, b, 0, 3, v_xm, a_xmh, p_k, b)
                if A:
                    silu(("A", 0), a, it)
                if B:
                    mix_hi(mix, b, 1, 3, v_xm, a_xmh, p_v, b)
                if A:
                    hidden_hi(("A", 0), a, [(p_dn[1], d + 1)])
                if C_:
                    relu(c, 0, it)
                if B:
                    mix_hi(mix, b, 2, 3, v_xm, a_xmh, p_r, b)
                if C_:
                    free = [(p_dn[0], b + 1 if B else NC), (p_dn[1], d + 1)]
                    for g in range(1, HP):
                        relu(c, g, it)
                        hidden_hi(("M", g - 1), c, free)
                    hidden_hi(("M", HP - 1), c, free)
                if B:
                    act.wait_ge(v_ng, b + 1)
                    need(act, v_dn, b)
                    act.activation(ex[:, 0], ng, ACT.Relu, scale=-1.0)
                    act.activation(ex[:, 1], ng, ACT.Relu).then_inc(a_re, 1)
                    act.wait_ge(a_re, 2 * b + 1)
                    act.activation(ex[:, 0:2], ex[:, 0:2], ACT.Exp, scale=-1.0).then_inc(a_ex, 1)
                    for f in range(KC):
                        act.activation(ex[:, 2, f], ng[:, f], ACT.Relu, bias=upw[:, f:f + 1], scale=-1.0)
                        ins = act.activation(ex[:, 3, f], ng[:, f], ACT.Relu, bias=nupw[:, f:f + 1])
                    ins.then_inc(a_re, 1)
                    act.wait_ge(a_re, 2 * b + 2)
                    act.activation(ex[:, 2:4], ex[:, 2:4], ACT.Exp, scale=-1.0).then_inc(a_ex, 1)
                    act.wait_ge(p_r, b + 1)
                    need(act, v_de, b)
                    act.activation(flat(er), flat(bankC), ACT.Exp, scale=-1.0).then_inc(a_er, 1)
                free = [(p_cv, c + 1)] if C_ else [(p_dn[0], a)]
                if A:
                    silu(("A", 1), a, it)
                if C_:
                    normalise(3, c, z03_tok, x3, [(p_t[0], a + 1) if A else (p_t[3], c)])
                if A:
                    hidden_hi(("A", 1), a, free)
                    if A and not B:
                        decode(NGU, NSL)
                    silu(("A", 2), a, it)
                if C_:
                    act.wait_ge(p_t[3], c + 1)
                    need(act, p_gu[1], upto(IP, IP - 1, c))
                    split_hi(z3[0][:], bankT[:]).then_inc(a_zh[3], 1)
                if A:
                    hidden_hi(("A", 2), a, free)
                    if A and not B:
                        split_raws()
                if B:
                    act.wait_ge(v_at, b + 1)
                    need(act, p_wo, b)
                    split_hi(att[0][:], n1).then_inc(a_ath, 1)
                if C_:
                    silu(("C", 0), c, it)
                    hidden_hi(("C", 0), c, free)
                    silu(("C", 1), c, it)
                if B:
                    normalise(2, b, z12_tok, x2, [(p_t[1], b + 1)])
                if C_:
                    hidden_hi(("C", 1), c, free)
                    silu(("C", 2), c, it)

            def mix_hi(operand, c, j, per, ready, done, free_sem, count):
                act.wait_ge(ready, upto(per, j, c + 1))
                need(act, free_sem, count)
                split_hi(operand[0][:, j], xm3(j % 2)).then_inc(done, 1)

            def silu(tile, c, it):
                s, i = "AC".index(tile[0]), TILES.index(tile)
                act.wait_ge(p_gu[s], upto(IP, tile[1], c + 1))
                wait_slot(act, SLOTS, tile, it, product_of)
                act.activation(sil[:, SLOTS[i]], flat(gu[BANKS[i]][0]), ACT.Silu).then_inc(a_sil[s], 1)

            def relu(c, g, it):
                act.wait_ge(p_ck, upto(HP, g, c + 1))
                wait_slot(act, SLOTS, ("M", g), it, product_of)
                act.activation(sil[:, SLOTS[TILES.index(("M", g))]], flat(ck_bank(g)), ACT.Relu).then_inc(a_rl, 1)

            def hidden_hi(tile, c, free):
                stage, p = tile
                per, ready, done = {"A": (IP, v_h[0], a_hh[0]), "C": (IP, v_h[1], a_hh[1]), "M": (HP, v_h2, a_h2h)}[stage]
                act.wait_ge(ready, upto(per, p, c + 1))
                for fs, fv in free:
                    need(act, fs, fv)
                whole = hval[:, SLOTS[TILES.index(tile)]].rearrange("p (a b) -> p a b", a=2)
                split_hi(hid[0][:, hid_pair(tile)], whole).then_inc(done, 1)

            def xm3(j):
                return xm[:, j].rearrange("p (a b) -> p a b", a=2)

            act.wait_ge(l_par, 16)
            act.activation(wdec[:], par[:, PARAMS.index("time_decay"), :], ACT.Exp).then_inc(a_dec, 1)
            act.wait_ge(l_lut, 16)
            act.wait_ge(v_lutd, 1)
            iteration(0, True, False, False, False)
            act.wait_ge(v_clear, 1)
            act.wait_ge(v_init, 3)
            iteration(1, True, True, False, False)
            iteration(2, True, True, True, False)
            iteration(3, True, True, True, True)
            with act.Fori(LOOP0, LOOP1) as it:
                iteration(it, True, True, True, True)
            iteration(NC, False, True, True, True)
            iteration(NC + 1, False, False, True, True)
            iteration(NC + 2, False, False, False, True)

        @block.vector
        def _(dve):
            def lo(dst, whole, hi):
                return dve.tensor_tensor(dst, whole, hi.bitcast(F32), ALU.subtract)

            def prologue():
                dve.wait_ge(l_lut, 16)
                dve.tensor_tensor(lutd[:], lutb[:, 1:LUT:2], lutb[:, 0:LUT:2], ALU.subtract).then_inc(v_lutd, 1)
                dve.wait_ge(g_ident, 2)

            def constants():
                dve.wait_ge(a_dec, 1)
                dve.tensor_scalar(wdec[:], wdec[:], -1.0, None, ALU.mult).then_inc(v_init, 1)
                dve.wait_ge(v_init, 1)
                dve.tensor_tensor(upw[:], wdec[:], par[:, PARAMS.index("time_first"), :], ALU.add).then_inc(v_init, 1)
                dve.wait_ge(v_init, 2)
                dve.tensor_scalar(nupw[:], upw[:], -1.0, None, ALU.mult).then_inc(v_init, 1)

            def decode(n0, n1):
                def bit(n):
                    idx, _, _, cols, loaded = slices[n]
                    dve.wait_ge(loaded, 32)
                    need(dve, a_leaf, n - 1)
                    need(dve, g_leaf, n - 1)
                    dve.tensor_scalar(two(bit0[n % 2], cols), idx, 1, None, ALU.bitwise_and).then_inc(v_bit, 1)

                bit(n0)
                for n in range(n0, n1):
                    idx, _, _, cols, _ = slices[n]
                    if n + 1 < n1:
                        bit(n + 1)
                    tree = leaves[n % 2]
                    for lev in range(3):
                        m = 3 * n + lev
                        need(dve, v_sel, m)
                        dve.tensor_scalar(two(mask, cols), idx, 2 << lev, None, ALU.bitwise_and).then_inc(v_mask, 1)
                        dve.wait_ge(v_mask, m + 1)
                        if lev == 0:
                            dve.wait_ge(a_leaf, n + 1)
                            dve.wait_ge(g_leaf, n + 1)
                        st = 1 << lev
                        dve.copy_predicated(tree[:, 0:8:2 * st, 0:2 * cols],
                                            mask[:, 0:2 * cols].unsqueeze(1).to_broadcast([P, 4 >> lev, 2 * cols]),
                                            tree[:, st:8:2 * st, 0:2 * cols]).then_inc(v_sel, 1)

            def split_raws():
                for n, (raw, hi, lo_) in enumerate(raws):
                    dve.wait_ge(a_raw, n + 1)
                    lo(lo_, raw, hi).then_inc(v_raw, 1)

            def clear():
                dve.wait_ge(a_whi, NSL)
                dve.wait_ge(g_wlo, NSL)
                dve.memset(xn1[:, :, CT:CT + 1], 0.0)
                dve.memset(xn2[:, :, CT:CT + 1], 0.0)
                dve.memset(state[:, 0, :, CT:CT + 1], NEG_INF)
                dve.memset(state[:, 1:3, :, CT:CT + 1], 0.0).then_inc(v_clear, 1)
                dve.wait_ge(v_clear, 1)

            def stats(k, c, src):
                for t in range(TT):
                    ins = dve.bn_stats(st6[:, k, t, :], src[:, t, :])
                ins.then_inc(v_st[k], 1)
                dve.wait_ge(g_ident, 2)
                dve.wait_ge(v_st[k], c + 1)
                need(dve, g_rs[k], c)
                for t in range(TT):
                    ins = dve.bn_aggr(mv[:, k, t, :], st6[:, k, t, :])
                ins.then_inc(v_mv[k], 1)

            def product(tile, c, it):
                s, i = "AC".index(tile[0]), TILES.index(tile)
                dve.wait_ge(a_sil[s], upto(IP, tile[1], c + 1))
                wait_slot(dve, SLOTS, tile, it, lo_of)
                dve.tensor_tensor(hval[:, SLOTS[i]], sil[:, SLOTS[i]], flat(gu[BANKS[i]][1]), ALU.mult).then_inc(v_h[s], 1)

            def relu_square(c, g, it):
                q = SLOTS[TILES.index(("M", g))]
                dve.wait_ge(a_rl, upto(HP, g, c + 1))
                wait_slot(dve, SLOTS, ("M", g), it, lo_of)
                dve.tensor_tensor(hval[:, q], sil[:, q], flat(ck_bank(g)), ALU.mult).then_inc(v_h2, 1)

            def wkv_state(b):
                dve.tensor_copy(state[:, :, :, 0:1], state[:, :, :, CT:CT + 1]).then_inc(v_cyw, 1)
                dve.wait_ge(v_cyw, b + 1)
                dve.wait_ge(p_k, b + 1)
                for f in range(KC):
                    ins = dve.tensor_tensor_scan(state[:, 0, f, 1:CT + 1], wdec[:, f:f + 1].to_broadcast([P, CT]), bankA[:, f, :],
                                                 state[:, 0, f, 0:1], ALU.add, ALU.max)
                ins.then_inc(v_pp, 1)
                dve.wait_ge(v_pp, b + 1)
                need(dve, a_re, 2 * b)
                for f in range(KC):
                    ins = dve.scalar_tensor_tensor(ng[:, f], state[:, 0, f, 0:CT], wdec[:, f:f + 1], bankA[:, f, :],
                                                   ALU.add, ALU.subtract)
                ins.then_inc(v_ng, 1)

            def wkv_scans(b):
                dve.wait_ge(a_ex, 2 * b + 1)
                dve.wait_ge(p_v, b + 1)
                need(dve, v_at, b)
                dve.tensor_tensor(kv_m, ex[:, 1], bankB[:], ALU.mult).then_inc(v_m, 1)
                dve.wait_ge(v_m, b + 1)
                for f in range(KC):
                    for j, add in ((1, kv_m[:, f]), (2, ex[:, 1, f])):
                        ins = dve.tensor_tensor_scan(state[:, j, f, 1:CT + 1], ex[:, 0, f], add, state[:, j, f, 0:1],
                                                     ALU.mult, ALU.add)
                ins.then_inc(v_ab, 1)

            def wkv_new(b):
                dve.wait_ge(a_ex, 2 * b + 2)
                need(dve, v_atl, b)
                need(dve, a_ath, b)
                dve.tensor_tensor(n2, ex[:, 3], bankB[:], ALU.mult).then_inc(v_n2, 1)

            def wkv_sums(b):
                dve.wait_ge(v_ab, b + 1)
                dve.tensor_tensor(n1, ex[:, 2], state[:, 1, :, 0:CT], ALU.mult).then_inc(v_n1, 1)
                dve.tensor_tensor(kv_m, ex[:, 2], state[:, 2, :, 0:CT], ALU.mult).then_inc(v_d1, 1)
                dve.wait_ge(v_d1, b + 1)
                dve.tensor_tensor(n1, n1, n2, ALU.add).then_inc(v_n, 1)
                dve.tensor_tensor(kv_m, kv_m, ex[:, 3], ALU.add).then_inc(v_dn, 1)

            def wkv_ratio(b):
                dve.wait_ge(v_dn, b + 1)
                dve.scalar_tensor_tensor(n2, er, 1.0, kv_m, ALU.add, ALU.mult).then_inc(v_de, 1)
                dve.wait_ge(v_de, b + 1)
                dve.reciprocal(kv_m, n2).then_inc(v_rc, 1)
                dve.wait_ge(v_rc, b + 1)
                dve.tensor_tensor(n1, n1, kv_m, ALU.mult).then_inc(v_at, 1)

            def mix_whole(src, j, name, free, done):
                for s, v in free:
                    need(dve, s, v)
                for f in range(KC):
                    ins = dve.scalar_tensor_tensor(xm[:, j % 2, f * CT:(f + 1) * CT], dx[:, f], pcol(name, f),
                                                   src[:, f, 0:CT], ALU.mult, ALU.add)
                ins.then_inc(done, 1)

            def mix_lo(operand, c, j, per, whole, hi, done):
                dve.wait_ge(whole, upto(per, j, c + 1))
                dve.wait_ge(hi, upto(per, j, c + 1))
                lo(operand[1][:, j], xm[:, j % 2].rearrange("p (a b) -> p a b", a=2), operand[0][:, j]).then_inc(done, 1)

            def cmix_whole(c, j):
                n = upto(3, 2 - j, c + 1)
                mix_whole(xn2, j, ("cmr", "cmk")[j], [(v_xml, n), (a_xmh, n)], v_cm)

            def tmix_whole(b, j):
                if j < 2:
                    free = [(v_cml, upto(2, j, b)), (a_cmh, upto(2, j, b))]
                else:
                    free = [(v_xml, upto(3, 0, b + 1)), (a_xmh, upto(3, 0, b + 1))]
                mix_whole(xn1, j, ("tmk", "tmv", "tmr")[j], free, v_xm)

            def iteration(it, A, B, C_, D):
                a, b, c, d = it, it - 1, it - 2, it - 3
                if D:
                    product(("C", 2), d, it - 1)
                if A:
                    dve.wait_ge(s_x, 16 * (a + 1))
                    stats(0, a, x_in)
                if C_:
                    dve.wait_ge(a_xn2, c + 1)
                    need(dve, v_xm, upto(3, 2, c + 1))
                    dve.tensor_tensor(dx, xn2[:, :, 1:CT + 1], xn2[:, :, 0:CT], ALU.subtract).then_inc(v_dx2, 1)
                    dve.wait_ge(v_dx2, c + 1)
                    cmix_whole(c, 0)
                    cmix_whole(c, 1)
                    mix_lo(cmix, c, 0, 2, v_cm, a_cmh, v_cml)
                if D:
                    dve.wait_ge(p_dn[1], d + 1)
                    need(dve, s_out, 16 * d)
                    dve.scalar_tensor_tensor(out_sb, bankC[:], 0.5, x3, ALU.mult, ALU.add).then_inc(v_out, 1)
                if A:
                    dve.wait_ge(a_zh[0], a + 1)
                    lo(z0[1][:], bankT[:], z0[0][:]).then_inc(v_zl[0], 1)
                if C_:
                    mix_lo(cmix, c, 1, 2, v_cm, a_cmh, v_cml)
                if A and not B:
                    decode(0, NGU)
                if B:
                    dve.wait_ge(a_xn1, b + 1)
                    need(dve, v_cm, upto(2, 1, b))
                    dve.tensor_tensor(dx, xn1[:, :, 1:CT + 1], xn1[:, :, 0:CT], ALU.subtract).then_inc(v_dx1, 1)
                    dve.wait_ge(v_dx1, b + 1)
                    tmix_whole(b, 0)
                    tmix_whole(b, 1)
                    mix_lo(mix, b, 0, 3, v_xm, a_xmh, v_xml)
                if A:
                    product(("A", 0), a, it)
                if B:
                    mix_lo(mix, b, 1, 3, v_xm, a_xmh, v_xml)
                if C_:
                    relu_square(c, 0, it)
                if B:
                    tmix_whole(b, 2)
                if C_:
                    relu_square(c, 1, it)
                if B:
                    mix_lo(mix, b, 2, 3, v_xm, a_xmh, v_xml)
                if C_:
                    relu_square(c, 2, it)
                    relu_square(c, 3, it)
                if B:
                    wkv_state(b)
                    wkv_scans(b)
                if C_:
                    dve.wait_ge(p_cv, c + 1)
                    dve.scalar_tensor_tensor(th, th, 1.0, bankA[:], ALU.add, ALU.mult).then_inc(v_t3, 1)
                    dve.wait_ge(v_t3, c + 1)
                    dve.wait_ge(g_x12, c + 1)
                    need(dve, v_out, d + 1)
                    dve.scalar_tensor_tensor(x3, th, 0.5, x12, ALU.mult, ALU.add).then_inc(v_x3, 1)
                    dve.wait_ge(v_x3, c + 1)
                    stats(3, c, x3)
                if B:
                    wkv_new(b)
                if A:
                    product(("A", 1), a, it)
                    if A and not B:
                        decode(NGU, NSL)
                if B:
                    wkv_sums(b)
                if A:
                    product(("A", 2), a, it)
                    if A and not B:
                        split_raws()
                if C_:
                    dve.wait_ge(a_zh[3], c + 1)
                    lo(z3[1][:], bankT[:], z3[0][:]).then_inc(v_zl[3], 1)
                if B:
                    wkv_ratio(b)
                    dve.wait_ge(a_ath, b + 1)
                    lo(att[1][:], n1, att[0][:]).then_inc(v_atl, 1)
                if A:
                    dve.wait_ge(p_dn[0], a + 1)
                    need(dve, g_x1k, b + 1)
                    need(dve, a_z[1], b + 1)
                    dve.scalar_tensor_tensor(x1[:], bankB[:], 0.5, x_in[:], ALU.mult, ALU.add).then_inc(v_x1, 1)
                    dve.wait_ge(v_x1, a + 1)
                    stats(1, a, x1)
                if C_:
                    product(("C", 0), c, it)
                if B:
                    dve.wait_ge(p_wo, b + 1)
                    dve.wait_ge(g_y, b + 1)
                    need(dve, g_x12, c + 1)
                    dve.tensor_tensor(x2, bankA[:], y, ALU.add).then_inc(v_x2, 1)
                    dve.wait_ge(v_x2, b + 1)
                    stats(2, b, x2)
                if C_:
                    product(("C", 1), c, it)

            prologue()
            constants()
            iteration(0, True, False, False, False)
            clear()
            iteration(1, True, True, False, False)
            iteration(2, True, True, True, False)
            iteration(3, True, True, True, True)
            with dve.Fori(LOOP0, LOOP1) as it:
                iteration(it, True, True, True, True)
            iteration(NC, False, True, True, True)
            iteration(NC + 1, False, False, True, True)
            iteration(NC + 2, False, False, False, True)

        @block.gpsimd
        def _(pool):
            def rsqrt(k, c):
                pool.wait_ge(v_mv[k], c + 1)
                need(pool, a_z[k], c)
                pool.tensor_tensor(veps[:, k], mv[:, k, :, 1], eps[:], ALU.add).then_inc(g_ve[k], 1)
                pool.wait_ge(g_ve[k], c + 1)
                scale, shift = (rstd[:, k], nbias[:, k]) if k != 1 else (y_scale[0][:], y_scale[1][:])
                if k == 1:
                    need(pool, g_y, c)
                pool.tensor_tensor(scale, veps[:, k], mhalf[:], ALU.pow).then_inc(g_pw[k], 1)
                pool.wait_ge(g_pw[k], c + 1)
                pool.tensor_tensor(veps[:, k], mv[:, k, :, 0], scale, ALU.mult).then_inc(g_mr[k], 1)
                pool.wait_ge(g_mr[k], c + 1)
                pool.tensor_tensor(shift, veps[:, k], minus[:], ALU.mult).then_inc(g_rs[k] if k != 1 else g_chain, 1)

            def second_norm(c):
                s1 = y_scale[0][:]
                n = 5 * c
                pool.wait_ge(g_chain, n + 1)
                pool.tensor_tensor(tmp2[:, 0], s1, s1, ALU.mult).then_inc(g_chain, 1)
                pool.wait_ge(g_chain, n + 2)
                pool.tensor_tensor(tmp2[:, 1], tmp2[:, 0], mv[:, 1, :, 1], ALU.mult).then_inc(g_chain, 1)
                pool.wait_ge(g_chain, n + 3)
                pool.tensor_tensor(tmp2[:, 0], tmp2[:, 1], eps[:], ALU.add).then_inc(g_chain, 1)
                pool.wait_ge(g_chain, n + 4)
                pool.tensor_tensor(tmp2[:, 1], tmp2[:, 0], mhalf[:], ALU.pow).then_inc(g_chain, 1)
                pool.wait_ge(g_chain, n + 5)
                pool.tensor_tensor(rstd[:, 1], tmp2[:, 1], s1, ALU.mult).then_inc(g_s2, 1)
                pool.tensor_tensor(nbias[:, 1], tmp2[:, 1], y_scale[1][:], ALU.mult).then_inc(g_rs[1], 1)

            def hidden_lo(tile, c):
                stage, p = tile
                per, ready, done = {"A": (IP, a_hh[0], g_hl[0]), "C": (IP, a_hh[1], g_hl[1]), "M": (HP, a_h2h, g_h2l)}[stage]
                pool.wait_ge(ready, upto(per, p, c + 1))
                whole = hval[:, SLOTS[TILES.index(tile)]].rearrange("p (a b) -> p a b", a=2)
                pool.tensor_tensor(hid[1][:, hid_pair(tile)], whole, hid[0][:, hid_pair(tile)].bitcast(F32),
                                   ALU.subtract).then_inc(done, 1)

            def decode(n0, n1):
                def lo_of_slice(n):
                    _, hi, lo_, cols, _ = slices[n]
                    pool.wait_ge(a_whi, n + 1)
                    pool.tensor_tensor(lo_, two(leaves[n % 2][:, 0], cols), hi.bitcast(F32), ALU.subtract).then_inc(g_wlo, 1)

                for n in range(n0, n1):
                    cols = slices[n][3]
                    pool.wait_ge(v_bit, n + 1)
                    need(pool, a_whi, n - 1)
                    for j in range(ACT_LEAVES, 8):
                        ins = pool.tensor_scalar(leaves[n % 2][:, j, 0:2 * cols], bit0[n % 2][:, 0:2 * cols],
                                                 lutd[:, j:j + 1], lutb[:, 2 * j:2 * j + 1], ALU.mult, ALU.add)
                    ins.then_inc(g_leaf, 1)
                    if n > n0:
                        lo_of_slice(n - 1)
                lo_of_slice(n1 - 1)

            def iteration(it, A, B, C_, D):
                a, b, c, d = it, it - 1, it - 2, it - 3
                if D:
                    hidden_lo(("C", 2), d)
                if A:
                    rsqrt(0, a)
                    if A and not B:
                        decode(0, NGU)
                    hidden_lo(("A", 0), a)
                if C_:
                    for g in range(HP):
                        hidden_lo(("M", g), c)
                    pool.wait_ge(v_x2, c + 1)
                    need(pool, v_x3, c)
                    pool.tensor_tensor(x12, x2, x1k, ALU.add).then_inc(g_x12, 1)
                if B:
                    before = c + 1 if isinstance(it, int) else pool.snap(c + 1)
                    pool.wait_ge(g_ident, 2)
                    need(pool, g_x12, before)
                    pool.tensor_scalar(x1k, x1[:], 1.0, 0.0, ALU.mult, ALU.add).then_inc(g_x1k, 1)
                    pool.wait_ge(g_ident, 2)
                    need(pool, v_x2, before)
                    for t in range(TT):
                        ins = pool.tensor_scalar(y[:, t], x1[:, t], y_scale[0][:, t:t + 1], y_scale[1][:, t:t + 1],
                                                 ALU.mult, ALU.add)
                    ins.then_inc(g_y, 1)
                if C_:
                    rsqrt(3, c)
                if A:
                    hidden_lo(("A", 1), a)
                    if A and not B:
                        decode(NGU, NSL)
                    hidden_lo(("A", 2), a)
                if C_:
                    hidden_lo(("C", 0), c)
                if B:
                    rsqrt(2, b)
                if A:
                    rsqrt(1, a)
                    second_norm(a)
                if C_:
                    hidden_lo(("C", 1), c)

            idx_last = idx_dn[:, KI - 1, :]
            pool.memset(idx_last, 0).then_inc(g_clear, 1)
            for const, value in ((mhalf, -0.5), (eps, EPS), (minus, -1.0)):
                pool.memset(const[:], value)
            for w in (*w_gate, *w_up):
                pool.memset(w[:, :, I:IPAD].bitcast(F32), 0.0)
            pool.memset(ident[:], 0.0).then_inc(g_ident, 1)
            pool.wait_ge(g_ident, 1)
            pool.affine_select(out=ident[:], in_=ident[:], compare_op=ALU.not_equal, fill=1.0, base=0,
                               pattern=[[-1, P]], channel_multiplier=1).then_inc(g_ident, 1)
            pool.wait_ge(v_lutd, 1)
            pool.wait_ge(g_ident, 2)
            iteration(0, True, False, False, False)
            pool.wait_ge(v_clear, 1)
            iteration(1, True, True, False, False)
            iteration(2, True, True, True, False)
            iteration(3, True, True, True, True)
            with pool.Fori(LOOP0, LOOP1) as it:
                iteration(it, True, True, True, True)
            iteration(NC, False, True, True, True)
            iteration(NC + 1, False, False, True, True)
            iteration(NC + 2, False, False, False, True)

        return nc


def kernel(**inputs):
    import numpy as np
    import concourse.bacc as bacc
    from concourse.bass_utils import run_bass_kernel_spmd

    def tiles(w):
        r, c = w.shape
        return np.ascontiguousarray(w.reshape(r // P, P, c).transpose(1, 0, 2))

    def get(name):
        return np.asarray(inputs["L0_" + name])

    params = np.stack([get("attn_" + n) for n in PARAMS]).reshape(len(PARAMS), KC, P).transpose(2, 0, 1)
    arrays = {
        "in_x": get("attn_x").reshape(T, C),
        "in_params": np.ascontiguousarray(params),
        "in_lut": np.ascontiguousarray(np.broadcast_to(get("ffn_lut"), (P, LUT))),
        "in_gate": tiles(get("ffn_gate_idx").T),
        "in_up": tiles(get("ffn_up_idx").T),
        "in_down": np.ascontiguousarray(get("ffn_down_idx").T),
        "in_square": np.ascontiguousarray(np.stack([tiles(get("attn_" + n).T) for n in SQUARE], axis=1)),
        "in_wck": tiles(get("attn_Wck").T),
        "in_wcv": tiles(get("attn_Wcv").T),
    }
    nc = bacc.Bacc("TRN2", target_bir_lowering=False, num_devices=1)
    args = [nc.dram_tensor(n, a.shape, mybir.dt.from_np(a.dtype), kind="ExternalInput").ap() for n, a in arrays.items()]
    out = nc.dram_tensor("out", (T, C), F32, kind="ExternalOutput").ap()
    build(nc, *args, out)
    r = run_bass_kernel_spmd(nc, [arrays], core_ids=[0])
    return r.results[0]["out"].reshape(1, T, C)
```

```python
from contextlib import ExitStack

import concourse.bass as bass
from concourse import mybir

P = 128
F32 = mybir.dt.float32
F32R = mybir.dt.float32r
I32 = mybir.dt.int32
ALU = mybir.AluOpType
ACT = mybir.ActivationFunctionType

T, C, I, H = 2048, 256, 688, 1024
EPS = 1e-5
NEG_INF = -1e38
CT = 256
NC = T // CT
TT = CT // P
KC = C // P
W = TT * C
IP = 3
KI = 2 * IP
ILAST = I - (KI - 1) * P
IFULL = (KI - 1) * P
UPROW = 64
assert ILAST <= UPROW and UPROW + ILAST <= P
KH = H // P
HP = KH // 2
HID = KH + 2
LUT = 16
PARAMS = ["ln1_w", "ln1_b", "ln2_w", "ln2_b", "time_decay", "time_first", "tmk", "tmv", "tmr", "cmk", "cmr"]
SQUARE = ["Wk", "Wv", "Wr", "Wo", "Wcr"]
LOOP0, LOOP1 = 4, NC


def need(eng, sem, value):
    if isinstance(value, int) and value <= 0:
        return
    eng.wait_ge(sem, value)


def upto(per, index, count):
    if isinstance(count, int) and count <= 0:
        return 0
    return per * (count - 1) + index + 1


def build(nc, x, params, lut, idx_gate, idx_up, idx_down, square, wck, wcv, out):
    with ExitStack() as ctx:
        def sb(name, shape, dt=F32):
            return ctx.enter_context(nc.sbuf_tensor(name, [P, *shape], dt))

        def sem(name):
            return ctx.enter_context(nc.semaphore(name))

        gu = [[ctx.enter_context(nc.psum_tensor(f"gu{i}{j}", [P, 2, CT], F32)) for j in range(2)] for i in range(2)]
        bankA = ctx.enter_context(nc.psum_tensor("bankA", [P, 2, CT], F32))
        bankB = ctx.enter_context(nc.psum_tensor("bankB", [P, 2, CT], F32))
        bankC = ctx.enter_context(nc.psum_tensor("bankC", [P, 2, CT], F32))
        bankT = ctx.enter_context(nc.psum_tensor("bankT", [P, 2, CT], F32))

        w_gate = [sb(f"w_gate{s}", [KC, IFULL + UPROW + ILAST], F32R) for s in ("_hi", "_lo")]
        w_up = [sb(f"w_up{s}", [KC, IFULL], F32R) for s in ("_hi", "_lo")]
        w_down = [sb(f"w_down{s}", [KI, C], F32R) for s in ("_hi", "_lo")]
        w_sq = [sb(f"w_sq{s}", [len(SQUARE), KC, C], F32R) for s in ("_hi", "_lo")]
        w_ck = [sb(f"w_ck{s}", [KC, H], F32R) for s in ("_hi", "_lo")]
        w_cv = [sb(f"w_cv{s}", [KH, C], F32R) for s in ("_hi", "_lo")]

        ident = sb("ident", [P])
        par = sb("par", [len(PARAMS), KC])
        lutb = sb("lutb", [LUT])
        lutd = sb("lutd", [LUT // 2])
        wdec = sb("wdec", [KC])
        upw = sb("upw", [KC])
        nupw = sb("nupw", [KC])
        mhalf, eps, minus = sb("mhalf", [TT]), sb("eps", [TT]), sb("minus", [TT])

        x_in = sb("x_in", [TT, C])
        z03_tok = sb("z03_tok", [TT, C])
        z12_tok = sb("z12_tok", [TT, C])
        z0 = [sb(f"z0{s}", [KC, CT], F32R) for s in ("_hi", "_lo")]
        sil = sb("sil", [2, W])
        hval = sb("hval", [2, W])
        hid = [sb(f"hid{s}", [HID, CT], F32R) for s in ("_hi", "_lo")]
        x1 = sb("x1", [TT, C])
        EARLY = len(SQUARE) * W + KC * H + KH * C + W
        with nc.sbuf_tensor("early", [P, EARLY], F32) as early:
            pass
        mix = [sb(f"mix{s}", [3, KC, CT], F32R) for s in ("_hi", "_lo")]
        cmix = [sb(f"cmix{s}", [2, KC, CT], F32R) for s in ("_hi", "_lo")]
        att = [sb(f"att{s}", [KC, CT], F32R) for s in ("_hi", "_lo")]
        z3 = [sb(f"z3{s}", [KC, CT], F32R) for s in ("_hi", "_lo")]
        st6 = sb("st6", [4, TT, 6])
        mv = sb("mv", [4, TT, 2])
        veps = sb("veps", [4, TT])
        rstd = sb("rstd", [4, TT])
        nbias = sb("nbias", [4, TT])
        warm = sb("warm", [TT])
        nmean = sb("nmean", [4, TT])
        veps2, scale2, shift2 = (sb(n, [2, TT]) for n in ("veps2", "scale2", "shift2"))

        DECODE = 2 * KC * I + KI * C + 2 * 8 * W
        region = sb("region", [DECODE])
        mask1 = sb("mask1", [TT, C])
        at = [0]

        def take(*shape):
            n = 1
            for s in shape:
                n *= s
            v = region[:, at[0]:at[0] + n]
            at[0] += n
            if len(shape) == 2:
                v = v.rearrange("p (a b) -> p a b", a=shape[0])
            if len(shape) == 3:
                v = v.rearrange("p (a b c) -> p a b c", a=shape[0], b=shape[1])
            return v

        idx_gu = take(2, KC, I).bitcast(I32)
        idx_dn = take(KI, C).bitcast(I32)
        leaves = [take(8, W), take(8, W)]
        bit0 = [z12_tok[:].rearrange("p a b -> p (a b)").bitcast(I32), early[:, len(SQUARE) * W:(len(SQUARE) + 1) * W].bitcast(I32)]
        mask = [t.rearrange("p a b -> p (a b)").bitcast(I32) for t in (x1[:], mask1[:], z03_tok[:])]
        mask_first = hval[:, 0].bitcast(I32)
        end = at[0]
        at[0] = 0
        xn1 = take(KC, CT + 1)
        xn2 = take(KC, CT + 1)
        dx = take(KC, CT)
        xm = take(2, W)
        state = take(3, KC, CT + 1)
        ng = take(KC, CT)
        ex = take(4, KC, CT)
        er = take(KC, CT)
        kv_m = take(KC, CT)
        n1 = take(KC, CT)
        n2 = take(KC, CT)
        y = take(TT, C)
        x1k = take(TT, C)
        x2 = take(TT, C)
        x12 = take(TT, C)
        th = take(TT, C)
        x3 = take(TT, C)
        out_sb = take(TT, C)
        assert at[0] <= end
        raw_sq = [early[:, j * W:(j + 1) * W].rearrange("p (a b) -> p a b", a=KC) for j in range(len(SQUARE))]
        at_ck, at_cv = (len(SQUARE) + 1) * W, (len(SQUARE) + 1) * W + KC * H
        raw_ck = [early[:, at_ck + k * H:at_ck + (k + 1) * H] for k in range(KC)]
        raw_cv = [early[:, at_cv + k * W:at_cv + (k + 1) * W].rearrange("p (a b) -> p a b", a=2) for k in range(KH // 2)]

        l_par, l_lut, l_dn, l_raw = (sem(f"l_{n}") for n in ("par", "lut", "dn", "raw"))
        l_idx = [[sem(f"l_{m}{p}") for m in ("gate", "up")] for p in range(IP)]
        s_x, s_out = sem("s_x"), sem("s_out")
        g_ident, g_clear, g_leaf, g_wlo, g_raw = (sem(f"g_{n}") for n in ("ident", "clear", "leaf", "wlo", "raw"))
        v_init, v_clear, v_lutd, v_bit, v_sel, v_wlo, v_raw = (sem(f"v_{n}") for n in ("init", "clear", "lutd", "bit", "sel", "wlo", "raw"))
        v_mask = [sem(f"v_mask{k}") for k in range(3)]
        a_leaf, a_whi, a_dec, a_raw = (sem(f"a_{n}") for n in ("leaf", "whi", "dec", "raw"))
        v_st, v_mv = [[sem(f"v_{n}{k}") for k in range(4)] for n in ("st", "mv")]
        g_ve, g_pw, g_rs = [[sem(f"g_{n}{k}") for k in range(4)] for n in ("ve", "pw", "rs")]
        g_mr = [sem(f"g_mr{k}") for k in range(4)]
        g_y, g_x12, g_x1k = sem("g_y"), sem("g_x12"), sem("g_x1k")
        a_z = [sem(f"a_z{k}") for k in range(4)]
        a_zh = {k: sem(f"a_zh{k}") for k in (0, 3)}
        v_zl = {k: sem(f"v_zl{k}") for k in (0, 3)}
        p_t = [sem(f"p_t{k}") for k in range(4)]
        p_gu, a_sil, v_h, a_hh, g_hl = ([sem(f"{n}{s}") for s in "AC"] for n in ("p_gu", "a_sil", "v_h", "a_hh", "g_hl"))
        p_dn = [sem(f"p_dn{s}") for s in "AC"]
        v_x1, v_out = sem("v_x1"), sem("v_out")
        a_cy1, a_xn1, v_dx1 = sem("a_cy1"), sem("a_xn1"), sem("v_dx1")
        v_xm, a_xmh, v_xml = sem("v_xm"), sem("a_xmh"), sem("v_xml")
        p_k, p_v, p_r = sem("p_k"), sem("p_v"), sem("p_r")
        v_cyw, v_pp, v_ng, a_er, a_re, a_ex = (sem(n) for n in ("v_cyw", "v_pp", "v_ng", "a_er", "a_re", "a_ex"))
        v_m, v_ab, v_n1, v_n2, g_d1, v_n, g_dn, v_de, v_rc, v_at, v_atl = (
            sem(n) for n in ("v_m", "v_ab", "v_n1", "v_n2", "g_d1", "v_n", "g_dn", "v_de", "v_rc", "v_at", "v_atl"))
        a_ath = sem("a_ath")
        p_wo, v_x2 = sem("p_wo"), sem("v_x2")
        a_cy2, a_xn2, v_dx2 = sem("a_cy2"), sem("a_xn2"), sem("v_dx2")
        v_cm, a_cmh, v_cml = sem("v_cm"), sem("a_cmh"), sem("v_cml")
        p_cr, a_th = sem("p_cr"), sem("a_th")
        p_ck, a_rl, v_h2, a_h2h, g_h2l = (sem(n) for n in ("p_ck", "a_rl", "v_h2", "a_h2h", "g_h2l"))
        p_cv, v_t3, v_x3 = sem("p_cv"), sem("v_t3"), sem("v_x3")

        def pcol(name, k):
            return par[:, PARAMS.index(name), k:k + 1]

        def flat(t):
            return t[:].rearrange("p a b -> p (a b)") if len(t.shape) == 3 else t

        def ck_bank(p):
            return gu[BANKS[TILES.index(("M", p))]][p % 2]

        TILES = [("M", 0), ("M", 1), ("M", 2), ("M", 3), ("A", 0), ("A", 1), ("A", 2), ("C", 0), ("C", 1), ("C", 2)]
        BANKS = [0, 0, 1, 1, 0, 1, 0, 1, 0, 1]
        SLOTS = [i % 2 for i in range(len(TILES))]
        PLACES = [1, 2, 3, 4, 0, 1, 2, 3, 4, 0]
        LAG = {"A": 0, "M": 2, "C": 2}

        def hid_at(stage, k):
            return 2 * PLACES[TILES.index((stage, k // 2))] + k % 2

        def hid_pair(tile):
            q = 2 * PLACES[TILES.index(tile)]
            return slice(q, q + 2)

        def last_user(slot_of, tile, it):
            i = TILES.index(tile)
            for back, js in ((0, range(i - 1, -1, -1)), (1, range(len(TILES) - 1, -1, -1))):
                for j in js:
                    c = it - back - LAG[TILES[j][0]]
                    there = 0 <= c < NC if isinstance(c, int) else True
                    if slot_of[j] == slot_of[i] and there:
                        return TILES[j], c
            return None

        def product_of(stage, p, count):
            return {"A": v_h[0], "C": v_h[1], "M": v_h2}[stage], upto(HP if stage == "M" else IP, p, count)

        def lo_of(stage, p, count):
            return {"A": g_hl[0], "C": g_hl[1], "M": g_h2l}[stage], upto(HP if stage == "M" else IP, p, count)

        def wait_slot(eng, slot_of, tile, it, done):
            before = last_user(slot_of, tile, it)
            if before is not None:
                (stage, p), c = before
                need(eng, *done(stage, p, c + 1))

        slices = []
        for p in range(IP):
            c0, c1 = p * 2 * P, min((p + 1) * 2 * P, I)
            whole = [(w_gate[i][:, :, c0:c1], 0, c1 - c0) for i in range(2)]
            slices.append((idx_gu[:, 0, :, c0:c1], [whole], c1 - c0, (l_idx[p][0], 16)))
            full = min(c1, IFULL)
            parts = [[(w_up[i][:, :, c0:full], 0, full - c0) for i in range(2)]]
            if full < c1:
                parts.append([(w_gate[i][:, :, IFULL + UPROW:], full - c0, c1 - c0) for i in range(2)])
            slices.append((idx_gu[:, 1, :, c0:c1], parts, c1 - c0, (l_idx[p][1], 16)))
        for p in range(IP):
            parts = [[(w_down[i][:, 2 * p:2 * p + 2, :], 0, C) for i in range(2)]]
            slices.append((idx_dn[:, 2 * p:2 * p + 2, :], parts, C, (l_dn, 32)))
        NSL = len(slices)
        ACT_LEAVES = 4
        raws = [(raw_sq[j], w_sq[0][:, j], w_sq[1][:, j]) for j in range(len(SQUARE))]
        raws += [(raw_ck[k], w_ck[0][:, k], w_ck[1][:, k]) for k in range(KC)]
        raws += [(raw_cv[k], w_cv[0][:, 2 * k:2 * k + 2], w_cv[1][:, 2 * k:2 * k + 2]) for k in range(KH // 2)]
        NRAW, NSQ = len(raws), len(SQUARE)
        POOL_SQ = 2
        BETWEEN = {4: 0, 6: 1, 7: 2}

        def two(t, cols, c0=0, c1=None):
            return t[:, 0:2 * cols].rearrange("p (k c) -> p k c", k=2)[:, :, c0:c1]

        block = ctx.enter_context(nc.Block())

        @block.sync
        def _(sp):
            sp.dma_start(lutb[:], lut).then_inc(l_lut, 16)

            def load_x(a):
                need(sp, v_x1, a)
                sp.dma_start(x_in[:], x[bass.ds(a * CT, CT), :].rearrange("(t p) c -> p t c", p=P)).then_inc(s_x, 16)

            for p in range(IP):
                c0, c1 = p * 2 * P, min((p + 1) * 2 * P, I)
                for m, idx in enumerate((idx_gate, idx_up)):
                    sp.dma_start(idx_gu[:, m, :, c0:c1], idx[:, :, c0:c1]).then_inc(l_idx[p][m], 16)
                if p == 0:
                    load_x(0)
                    sp.dma_start(par[:], params).then_inc(l_par, 16)
            sp.wait_ge(g_clear, 1)
            sp.dma_start(idx_dn[:, 0:KI - 1], idx_down[0:(KI - 1) * P].rearrange("(k p) c -> p k c", p=P)).then_inc(l_dn, 16)
            sp.dma_start(idx_dn[0:ILAST, KI - 1], idx_down[(KI - 1) * P:I]).then_inc(l_dn, 16)
            for j in range(len(SQUARE)):
                sp.dma_start(raw_sq[j], square[:, j]).then_inc(l_raw, 16)
            for k in range(KC):
                sp.dma_start(raw_ck[k], wck[:, k]).then_inc(l_raw, 16)
            for k in range(KH // 2):
                sp.dma_start(raw_cv[k], wcv[:, 2 * k:2 * k + 2]).then_inc(l_raw, 16)

            def store(d):
                sp.wait_ge(v_out, d + 1)
                sp.dma_start(out[bass.ds(d * CT, CT), :].rearrange("(t p) c -> p t c", p=P), out_sb).then_inc(s_out, 16)

            for a in range(1, LOOP0):
                load_x(a)
            store(0)
            with sp.Fori(LOOP0, LOOP1) as it:
                load_x(it)
                store(it - 3)
            for d in range(NC - 3, NC):
                store(d)
            sp.wait_ge(s_out, 16 * NC)

        @block.tensor
        def _(pe):
            def product(parts, lo_waits, terms):
                for half in range(2):
                    if half == 1:
                        for s, v in lo_waits:
                            pe.wait_ge(s, v)
                    for n, (o, weight, acts, stationary) in enumerate(terms):
                        for w, x in (((0, 0), (1, 0)) if half == 0 else ((0, 1),)):
                            l, m = (weight[w], acts[x]) if stationary == "weight" else (acts[x], weight[w])
                            first = half == 0 and n == 0 and w == 0 and parts[0]
                            last = half == 1 and n == len(terms) - 1 and parts[1]
                            mm = pe.matmul(o, l, m, start=first, stop=last, skip_group_check=True)
                return mm

            def feat(bank, weight, cols, acts):
                return [(bank[:, i, :], [u[:, k, c0:c0 + P] for u in weight], [h[:, k, :] for h in acts], "weight")
                        for i, c0 in enumerate(cols) for k in range(KC)]

            def tok(bank, weight, acts, tiles, rows=P):
                return [(bank[:, t, :], [u[0:rows, kw, :] for u in weight],
                         [h[0:rows, ka, t * P:(t + 1) * P] for h in acts], "acts")
                        for kw, ka in tiles for t in range(TT)]

            def transposes(k, c, src, free_sem, free_count):
                pe.wait_ge(a_z[k], c + 1)
                need(pe, free_sem, free_count)
                for t in range(TT):
                    for f in range(KC):
                        mm = pe.transpose(bankT[:, f, t * P:(t + 1) * P], src[:, t, f * P:(f + 1) * P], ident[:])
                mm.then_inc(p_t[k], 1)

            def time_mix(b, j):
                bank, done, free_sem, count = (
                    (bankA, p_k, a_th, b),
                    (bankB, p_v, v_x1, b + 1),
                    (bankC, p_r, v_out, b - 1))[j]
                pe.wait_ge(a_xmh, upto(3, j, b + 1))
                need(pe, free_sem, count)
                product((True, True), [(v_xml, upto(3, j, b + 1))],
                        feat(bank, [w[:, j] for w in w_sq], (0, P), [h[:, j] for h in mix])).then_inc(done, 1)

            def cv(c, free_sem, count):
                pe.wait_ge(free_sem, count)
                for g in range(HP):
                    pe.wait_ge(a_h2h, upto(HP, g, c + 1))
                    mm = product((g == 0, g == HP - 1), [(g_h2l, upto(HP, g, c + 1))],
                                 tok(bankA, w_cv, hid, [(k, hid_at("M", k)) for k in (2 * g, 2 * g + 1)]))
                mm.then_inc(p_cv, 1)

            def gate_up(tile, c, it):
                s, p = "AC".index(tile[0]), tile[1]
                bank, z = gu[BANKS[TILES.index(tile)]], (z0, z3)[s]
                wait_slot(pe, BANKS, tile, it, product_of)
                lo_waits = [(v_zl[(0, 3)[s]], c + 1)] if p == 0 else []
                cols = (2 * p * P, (2 * p + 1) * P)
                if p < IP - 1:
                    product((True, True), lo_waits, feat(bank[0], w_gate, cols, z))
                    mm = product((True, True), [], feat(bank[1], w_up, cols, z))
                else:
                    product((True, False), lo_waits, feat(bank[0], w_gate, cols[:1], z))
                    packed = [(bank[0][0:UPROW + ILAST, 1, :], [u[:, k, IFULL:] for u in w_gate], [h[:, k, :] for h in z],
                               "weight") for k in range(KC)]
                    product((False, True), [], packed)
                    mm = product((True, True), [], feat(bank[1], w_up, cols[:1], z))
                mm.then_inc(p_gu[s], 1)

            def down(s, c, bank, pairs):
                for p in pairs:
                    pe.wait_ge(a_hh[s], upto(IP, p, c + 1))
                    at = [(k, hid_at("AC"[s], k)) for k in (2 * p, 2 * p + 1)]
                    terms = tok(bank, w_down, hid, at) if p < IP - 1 else (
                        tok(bank, w_down, hid, at[:1]) + tok(bank, w_down, hid, at[1:], ILAST))
                    mm = product((p == 0, p == IP - 1), [lo_of("AC"[s], p, c + 1)], terms)
                if pairs[-1] == IP - 1:
                    mm.then_inc(p_dn[s], 1)

            def att_out(b, free_sem, count):
                pe.wait_ge(a_ath, b + 1)
                pe.wait_ge(free_sem, count)
                product((True, True), [(v_atl, b + 1)], tok(bankA, [w[:, 3] for w in w_sq], att, [(k, k) for k in range(KC)])
                        ).then_inc(p_wo, 1)

            def cr(c):
                pe.wait_ge(a_cmh, upto(2, 0, c + 1))
                pe.wait_ge(v_x2, c + 1)
                product((True, True), [(v_cml, upto(2, 0, c + 1))],
                        tok(bankA, [w[:, 4] for w in w_sq], [h[:, 0] for h in cmix], [(k, k) for k in range(KC)])
                        ).then_inc(p_cr, 1)

            def ck(c, g, it):
                if g == 0:
                    pe.wait_ge(a_cmh, upto(2, 1, c + 1))
                if g % 2 == 0:
                    wait_slot(pe, BANKS, ("M", g), it, product_of)
                product((True, True), [(v_cml, upto(2, 1, c + 1))] if g == 0 else [],
                        feat(ck_bank(g), w_ck, (2 * g * P, (2 * g + 1) * P), [h[:, 1] for h in cmix])).then_inc(p_ck, 1)

            def keep_warm(count, bank):
                for _ in range(count):
                    pe.matmul(bank[:, 0, :], w_gate[0][:, 0, 0:P], w_gate[0][:, 1, 0:CT], start=True, stop=True,
                              skip_group_check=True)

            def iteration(it, A, B, C_, D):
                a, b, c, d = it, it - 1, it - 2, it - 3
                first = B and not C_
                if D:
                    pe.wait_ge(a_er, c + 1 if C_ else NC)
                    down(1, d, bankC, range(IP))
                if B:
                    transposes(1, b, z12_tok, a_xn2, c + 1)
                    if first:
                        keep_warm(14, gu[1][1])
                if C_:
                    cr(c)
                    if not D:
                        pe.wait_ge(g_raw, POOL_SQ + NRAW - NSQ)
                    ck(c, 0, it)
                    ck(c, 1, it)
                if A:
                    transposes(0, a, z03_tok, a_xn1, b + 1)
                if C_:
                    ck(c, 2, it)
                    ck(c, 3, it)
                if B:
                    if first:
                        pe.wait_ge(g_raw, POOL_SQ)
                        pe.wait_ge(v_raw, NSQ - POOL_SQ)
                    time_mix(b, 0)
                if A:
                    if not B:
                        pe.wait_ge(a_whi, 2)
                        pe.wait_ge(g_wlo, 2)
                    pe.wait_ge(a_zh[0], a + 1)
                    gate_up(("A", 0), a, it)
                if B:
                    time_mix(b, 1)
                    time_mix(b, 2)
                if C_:
                    cv(c, *((v_ng, b + 1) if B else (a_th, c + 1)))
                    if not A:
                        keep_warm(46, gu[1][1])
                if A:
                    for p in (1, 2):
                        if not B:
                            pe.wait_ge(a_whi, 2 * p + 2)
                            pe.wait_ge(g_wlo, 2 * p + 2)
                        gate_up(("A", p), a, it)
                        if p == 1 and first:
                            keep_warm(30, bankT)
                    if B:
                        pe.wait_ge(v_n2, b + 1)
                    else:
                        pe.wait_ge(a_whi, NSL - 2)
                        pe.wait_ge(g_wlo, NSL - 2)
                    down(0, a, bankB, (0,))
                    if not B:
                        keep_warm(20, bankT)
                if C_:
                    transposes(3, c, z03_tok, *((v_zl[0], a + 1) if A else (a_xn1, NC) if B else (a_xn2, NC)))
                    if not A:
                        keep_warm(8, gu[1][1])
                if A:
                    if not B:
                        pe.wait_ge(a_whi, NSL - 1)
                        pe.wait_ge(g_wlo, NSL - 1)
                    down(0, a, bankB, (1,))
                    if not B:
                        keep_warm(20, bankT)
                if C_:
                    pe.wait_ge(a_zh[3], c + 1)
                    gate_up(("C", 0), c, it)
                if first:
                    att_out(b, v_ng, b + 1)
                if A:
                    if not B:
                        pe.wait_ge(a_whi, NSL)
                        pe.wait_ge(v_wlo, 1)
                    down(0, a, bankB, (2,))
                    if not B:
                        keep_warm(32, gu[1][1])
                    elif first:
                        keep_warm(20, gu[1][1])
                if B and not first:
                    att_out(b, v_t3, c + 1)
                if C_:
                    gate_up(("C", 1), c, it)
                    gate_up(("C", 2), c, it)
                if B:
                    transposes(2, b, z12_tok, *((v_zl[3], c + 1) if C_ else (v_zl[0], a + 1)))
                    if first:
                        keep_warm(14, gu[1][1])

            pe.wait_ge(g_ident, 2)
            iteration(0, True, False, False, False)
            iteration(1, True, True, False, False)
            iteration(2, True, True, True, False)
            iteration(3, True, True, True, True)
            with pe.Fori(LOOP0, LOOP1) as it:
                iteration(it, True, True, True, True)
            iteration(NC, False, True, True, True)
            iteration(NC + 1, False, False, True, True)
            iteration(NC + 2, False, False, False, True)

        @block.scalar
        def _(act):
            def split_hi(dst, src):
                return act.copy(dst, src)

            def split_raws(n0, n1):
                act.wait_ge(l_raw, 16 * NRAW)
                for raw, hi, _ in raws[n0:n1]:
                    split_hi(hi, raw).then_inc(a_raw, 1)

            def decode(before, after):
                def leaves_of(n):
                    cols = slices[n][2]
                    act.wait_ge(v_bit, n + 1)
                    need(act, v_sel, 3 * (n - 1))
                    for j in reversed(range(ACT_LEAVES)):
                        if j == 0:
                            need(act, g_wlo, n - 1)
                        ins = act.activation(leaves[n % 2][:, j, 0:2 * cols], bit0[n % 2][:, 0:2 * cols], ACT.Identity,
                                             bias=lutb[:, 2 * j:2 * j + 1], scale=lutd[:, j:j + 1])
                    ins.then_inc(a_leaf, 1)

                def hi_of(n):
                    _, parts, cols, _ = slices[n]
                    act.wait_ge(v_sel, 3 * (n + 1))
                    for (hi, c0, c1), _ in parts:
                        ins = split_hi(hi, two(leaves[n % 2][:, 0], cols, c0, c1))
                    ins.then_inc(a_whi, 1)

                leaves_of(0)
                before()
                leaves_of(1)
                after()
                for n in range(NSL):
                    if n == NSL - 1:
                        split_raws(0, NSQ)
                    hi_of(n)
                    if n in BETWEEN:
                        hidden_hi(("A", BETWEEN[n]), 0, [])
                    if n + 1 in BETWEEN:
                        silu(("A", BETWEEN[n + 1]), 0, 0)
                    if n + 2 < NSL:
                        leaves_of(n + 2)

            def normalise(k, c, dst, src, free):
                act.wait_ge(g_rs[k], c + 1)
                for s, v in free:
                    need(act, s, v)
                scale, shift = (rstd[:, k], nbias[:, k]) if k != 1 else (scale2[:, 1], shift2[:, 1])
                for t in range(TT):
                    ins = act.activation(dst[:, t, :], src[:, t, :], ACT.Identity, bias=shift[:, t:t + 1],
                                         scale=scale[:, t:t + 1])
                ins.then_inc(a_z[k], 1)

            def affine(k, c, xn, cy, done, wn, bn, free):
                for s, v in free:
                    need(act, s, v)
                act.copy(xn[:, :, 0:1], xn[:, :, CT:CT + 1]).then_inc(cy, 1)
                act.wait_ge(p_t[k], c + 1)
                act.wait_ge(cy, c + 1)
                for f in range(KC):
                    ins = act.activation(xn[:, f, 1:CT + 1], bankT[:, f, :], ACT.Identity, bias=pcol(bn, f), scale=pcol(wn, f))
                ins.then_inc(done, 1)

            def iteration(it, A, B, C_, D):
                a, b, c, d = it, it - 1, it - 2, it - 3
                first = B and not C_
                if C_:
                    affine(2, c, xn2, a_cy2, a_xn2, "ln2_w", "ln2_b", [(v_cm, upto(2, 1, c))])
                if D:
                    hidden_hi(("C", 2), d, [(p_dn[0], b + 1 if B else NC)])
                if B:
                    normalise(1, b, z12_tok, x1, [(p_t[2], c + 1)])
                if C_:
                    mix_hi(cmix, c, 0, 2, v_cm, a_cmh, p_cr, c)
                    mix_hi(cmix, c, 1, 2, v_cm, a_cmh, p_ck, HP * c)
                if B:
                    affine(1, b, xn1, a_cy1, a_xn1, "ln1_w", "ln1_b", [(v_xm, upto(3, 2, b))])
                if A:
                    normalise(0, a, z03_tok, x_in, [(p_t[3], d + 1)])
                if C_:
                    act.wait_ge(p_cr, c + 1)
                    need(act, v_x3, c)
                    act.activation(th, bankA[:], ACT.Tanh, scale=0.5).then_inc(a_th, 1)
                    relu(c, 0, it)
                if B:
                    mix_hi(mix, b, 0, 3, v_xm, a_xmh, p_k, b)
                free = [(p_dn[0], b + 1 if B else NC), (p_dn[1], d + 1)]
                if C_:
                    relu(c, 1, it)
                    hidden_hi(("M", 0), c, free)
                if A:
                    act.wait_ge(p_t[0], a + 1)
                    need(act, p_gu[0], upto(IP, IP - 1, a))
                    split_hi(z0[0][:], bankT[:]).then_inc(a_zh[0], 1)
                if B:
                    mix_hi(mix, b, 1, 3, v_xm, a_xmh, p_v, b)
                if C_:
                    relu(c, 2, it)
                    hidden_hi(("M", 1), c, free)
                if B:
                    mix_hi(mix, b, 2, 3, v_xm, a_xmh, p_r, b)
                if C_:
                    relu(c, 3, it)
                    hidden_hi(("M", 2), c, free)
                    hidden_hi(("M", 3), c, free)
                if A and not first:
                    silu(("A", 0), a, it)
                if B:
                    act.activation(warm[:], mhalf[:], ACT.Exp)
                    act.wait_ge(v_ng, b + 1)
                    need(act, g_dn, b)
                    act.activation(ex[:, 0], ng, ACT.Relu, scale=-1.0)
                    act.activation(ex[:, 1], ng, ACT.Relu).then_inc(a_re, 1)
                    act.wait_ge(a_re, 2 * b + 1)
                    act.activation(ex[:, 0:2], ex[:, 0:2], ACT.Exp, scale=-1.0).then_inc(a_ex, 1)
                    if A and not first:
                        hidden_hi(("A", 0), a, [(p_dn[1], d + 1)])
                    for f in range(KC):
                        act.activation(ex[:, 2, f], ng[:, f], ACT.Relu, bias=upw[:, f:f + 1], scale=-1.0)
                        ins = act.activation(ex[:, 3, f], ng[:, f], ACT.Relu, bias=nupw[:, f:f + 1])
                    ins.then_inc(a_re, 1)
                    act.wait_ge(a_re, 2 * b + 2)
                    act.activation(ex[:, 2:4], ex[:, 2:4], ACT.Exp, scale=-1.0).then_inc(a_ex, 1)
                    act.wait_ge(p_r, b + 1)
                    need(act, v_de, b)
                    act.activation(flat(er), flat(bankC), ACT.Exp, scale=-1.0).then_inc(a_er, 1)
                if first:
                    silu(("A", 0), a, it)
                    hidden_hi(("A", 0), a, [(p_dn[1], d + 1)])
                free = [(p_cv, c + 1)] if C_ else [(p_dn[0], a)]
                if A:
                    silu(("A", 1), a, it)
                if A:
                    hidden_hi(("A", 1), a, free)
                if C_:
                    normalise(3, c, z03_tok, x3, [(p_t[0], a + 1) if A else (p_t[3], c)])
                if A:
                    silu(("A", 2), a, it)
                if C_:
                    act.wait_ge(p_t[3], c + 1)
                    need(act, p_gu[1], upto(IP, IP - 1, c))
                    split_hi(z3[0][:], bankT[:]).then_inc(a_zh[3], 1)
                if A and not first:
                    hidden_hi(("A", 2), a, free)
                if B:
                    act.wait_ge(v_at, b + 1)
                    need(act, p_wo, b)
                    split_hi(att[0][:], n1).then_inc(a_ath, 1)
                if first:
                    hidden_hi(("A", 2), a, free)
                if C_:
                    silu(("C", 0), c, it)
                    hidden_hi(("C", 0), c, free)
                    silu(("C", 1), c, it)
                if B:
                    normalise(2, b, z12_tok, x2, [(p_t[1], b + 1)])
                if C_:
                    hidden_hi(("C", 1), c, free)
                    silu(("C", 2), c, it)

            def mix_hi(operand, c, j, per, ready, done, free_sem, count):
                act.wait_ge(ready, upto(per, j, c + 1))
                need(act, free_sem, count)
                split_hi(operand[0][:, j], xm3(j % 2)).then_inc(done, 1)

            def silu(tile, c, it):
                s, i = "AC".index(tile[0]), TILES.index(tile)
                act.wait_ge(p_gu[s], upto(IP, tile[1], c + 1))
                wait_slot(act, SLOTS, tile, it, product_of)
                gate = gu[BANKS[i]][0]
                if tile[1] < IP - 1:
                    act.activation(sil[:, SLOTS[i]], flat(gate), ACT.Silu).then_inc(a_sil[s], 1)
                else:
                    act.activation(sil[:, SLOTS[i], 0:CT], gate[:, 0, :], ACT.Silu)
                    act.activation(sil[0:ILAST, SLOTS[i], CT:], gate[0:ILAST, 1, :], ACT.Silu).then_inc(a_sil[s], 1)

            def relu(c, g, it):
                act.wait_ge(p_ck, upto(HP, g, c + 1))
                wait_slot(act, SLOTS, ("M", g), it, product_of)
                act.activation(sil[:, SLOTS[TILES.index(("M", g))]], flat(ck_bank(g)), ACT.Relu).then_inc(a_rl, 1)

            def hidden_hi(tile, c, free):
                stage, p = tile
                per, ready, done = {"A": (IP, v_h[0], a_hh[0]), "C": (IP, v_h[1], a_hh[1]), "M": (HP, v_h2, a_h2h)}[stage]
                act.wait_ge(ready, upto(per, p, c + 1))
                for fs, fv in free:
                    need(act, fs, fv)
                whole = hval[:, SLOTS[TILES.index(tile)]].rearrange("p (a b) -> p a b", a=2)
                split_hi(hid[0][:, hid_pair(tile)], whole).then_inc(done, 1)

            def xm3(j):
                return xm[:, j].rearrange("p (a b) -> p a b", a=2)

            act.wait_ge(l_lut, 16)
            act.activation(warm[:], lutb[:, 0:TT], ACT.Identity)
            act.wait_ge(v_lutd, 1)

            def before():
                normalise(0, 0, z03_tok, x_in, [])

            def after():
                act.wait_ge(p_t[0], 1)
                split_hi(z0[0][:], bankT[:]).then_inc(a_zh[0], 1)
                act.wait_ge(l_par, 16)
                act.activation(wdec[:], par[:, PARAMS.index("time_decay"), :], ACT.Exp).then_inc(a_dec, 1)

            decode(before, after)
            split_raws(NSQ, NRAW)
            act.wait_ge(v_clear, 1)
            act.wait_ge(v_init, 3)
            iteration(1, True, True, False, False)
            iteration(2, True, True, True, False)
            iteration(3, True, True, True, True)
            with act.Fori(LOOP0, LOOP1) as it:
                iteration(it, True, True, True, True)
            iteration(NC, False, True, True, True)
            iteration(NC + 1, False, False, True, True)
            iteration(NC + 2, False, False, False, True)

        @block.vector
        def _(dve):
            def lo(dst, whole, hi):
                return dve.tensor_tensor(dst, whole, hi.bitcast(F32), ALU.subtract)

            def prologue():
                dve.wait_ge(l_lut, 16)
                dve.tensor_tensor(lutd[:], lutb[:, 1:LUT:2], lutb[:, 0:LUT:2], ALU.subtract).then_inc(v_lutd, 1)
                dve.wait_ge(g_ident, 2)

            def constants():
                dve.wait_ge(a_dec, 1)
                dve.tensor_scalar(wdec[:], wdec[:], -1.0, None, ALU.mult).then_inc(v_init, 1)
                dve.wait_ge(v_init, 1)
                dve.tensor_tensor(upw[:], wdec[:], par[:, PARAMS.index("time_first"), :], ALU.add).then_inc(v_init, 1)
                dve.wait_ge(v_init, 2)
                dve.tensor_scalar(nupw[:], upw[:], -1.0, None, ALU.mult).then_inc(v_init, 1)

            def decode(before, after):
                def bit(n):
                    idx, _, cols, loaded = slices[n]
                    dve.wait_ge(*loaded)
                    need(dve, a_leaf, n - 1)
                    need(dve, g_leaf, n - 1)
                    dve.tensor_scalar(two(bit0[n % 2], cols), idx, 1, None, ALU.bitwise_and).then_inc(v_bit, 1)

                def mask_of(n, lev):
                    return mask_first if (n, lev) == (0, 2) else mask[lev]

                def take_mask(n, lev):
                    need(dve, v_sel, 3 * (n - 1) + lev + 1 if n else 0)
                    idx, _, cols, loaded = slices[n]
                    dve.wait_ge(*loaded)
                    dve.tensor_scalar(two(mask_of(n, lev), cols), idx, 2 << lev, None, ALU.bitwise_and).then_inc(v_mask[lev], 1)

                def choose(n, lev):
                    cols, tree, st = slices[n][2], leaves[n % 2], 1 << lev
                    dve.wait_ge(v_mask[lev], n + 1)
                    need(dve, v_sel, 3 * n + lev)
                    dve.copy_predicated(tree[:, 0:8:2 * st, 0:2 * cols],
                                        mask_of(n, lev)[:, 0:2 * cols].unsqueeze(1).to_broadcast([P, 4 >> lev, 2 * cols]),
                                        tree[:, st:8:2 * st, 0:2 * cols]).then_inc(v_sel, 1)

                bit(0)
                take_mask(0, 0)
                before()
                for n in range(NSL):
                    take_mask(n, 1)
                    if n + 1 < NSL:
                        bit(n + 1)
                    dve.wait_ge(a_leaf, n + 1)
                    dve.wait_ge(g_leaf, n + 1)
                    choose(n, 0)
                    if n == 1:
                        dve.wait_ge(p_t[0], 1)
                    take_mask(n, 2)
                    if n == 1:
                        after()
                    choose(n, 1)
                    if n + 1 < NSL:
                        take_mask(n + 1, 0)
                    choose(n, 2)
                    if n in BETWEEN:
                        product(("A", BETWEEN[n]), 0, 0)
                dve.wait_ge(a_whi, NSL)
                (hi, _, _), (lo_, _, _) = slices[NSL - 1][1][0]
                lo(lo_, two(leaves[(NSL - 1) % 2][:, 0], slices[NSL - 1][2]), hi).then_inc(v_wlo, 1)

            def split_squares(n0, n1):
                for n in range(n0, n1):
                    raw, hi, lo_ = raws[n]
                    dve.wait_ge(a_raw, n + 1)
                    lo(lo_, raw, hi).then_inc(v_raw, 1)

            def residual(a):
                dve.wait_ge(p_dn[0], a + 1)
                need(dve, g_x1k, a)
                need(dve, a_z[1], a)
                dve.scalar_tensor_tensor(x1[:], bankB[:], 0.5, x_in[:], ALU.mult, ALU.add).then_inc(v_x1, 1)

            def clear():
                dve.wait_ge(v_wlo, 1)
                dve.wait_ge(g_wlo, NSL - 1)
                dve.memset(xn1[:, :, CT:CT + 1], 0.0)
                dve.memset(xn2[:, :, CT:CT + 1], 0.0)
                dve.memset(state[:, 0, :, CT:CT + 1], NEG_INF)
                dve.memset(state[:, 1:3, :, CT:CT + 1], 0.0).then_inc(v_clear, 1)
                dve.wait_ge(v_clear, 1)

            def stats(k, c, src):
                for t in range(TT):
                    ins = dve.bn_stats(st6[:, k, t, :], src[:, t, :])
                ins.then_inc(v_st[k], 1)
                dve.wait_ge(g_ident, 2)
                dve.wait_ge(v_st[k], c + 1)
                need(dve, g_rs[k], c)
                for t in range(TT):
                    ins = dve.bn_aggr(mv[:, k, t, :], st6[:, k, t, :])
                ins.then_inc(v_mv[k], 1)

            def product(tile, c, it):
                s, i = "AC".index(tile[0]), TILES.index(tile)
                dve.wait_ge(a_sil[s], upto(IP, tile[1], c + 1))
                wait_slot(dve, SLOTS, tile, it, lo_of)
                gate, up = gu[BANKS[i]]
                h, g = hval[:, SLOTS[i]], sil[:, SLOTS[i]]
                if tile[1] < IP - 1:
                    dve.tensor_tensor(h, g, flat(up), ALU.mult).then_inc(v_h[s], 1)
                else:
                    dve.tensor_tensor(h[:, 0:CT], g[:, 0:CT], up[:, 0, :], ALU.mult)
                    dve.tensor_tensor(h[0:ILAST, CT:], g[0:ILAST, CT:], gate[UPROW:UPROW + ILAST, 1, :], ALU.mult
                                      ).then_inc(v_h[s], 1)

            def relu_square(c, g, it):
                q = SLOTS[TILES.index(("M", g))]
                dve.wait_ge(a_rl, upto(HP, g, c + 1))
                wait_slot(dve, SLOTS, ("M", g), it, lo_of)
                dve.tensor_tensor(hval[:, q], sil[:, q], flat(ck_bank(g)), ALU.mult).then_inc(v_h2, 1)

            def wkv_state(b):
                dve.tensor_copy(state[:, :, :, 0:1], state[:, :, :, CT:CT + 1]).then_inc(v_cyw, 1)
                dve.wait_ge(v_cyw, b + 1)
                dve.wait_ge(p_k, b + 1)
                for f in range(KC):
                    ins = dve.tensor_tensor_scan(state[:, 0, f, 1:CT + 1], wdec[:, f:f + 1].to_broadcast([P, CT]), bankA[:, f, :],
                                                 state[:, 0, f, 0:1], ALU.add, ALU.max)
                ins.then_inc(v_pp, 1)
                dve.wait_ge(v_pp, b + 1)
                need(dve, a_re, 2 * b)
                for f in range(KC):
                    ins = dve.scalar_tensor_tensor(ng[:, f], state[:, 0, f, 0:CT], wdec[:, f:f + 1], bankA[:, f, :],
                                                   ALU.add, ALU.subtract)
                ins.then_inc(v_ng, 1)

            def wkv_scans(b):
                dve.wait_ge(a_ex, 2 * b + 1)
                dve.wait_ge(p_v, b + 1)
                need(dve, v_at, b)
                dve.tensor_tensor(kv_m, ex[:, 1], bankB[:], ALU.mult).then_inc(v_m, 1)
                dve.wait_ge(v_m, b + 1)
                for f in range(KC):
                    for j, add in ((1, kv_m[:, f]), (2, ex[:, 1, f])):
                        ins = dve.tensor_tensor_scan(state[:, j, f, 1:CT + 1], ex[:, 0, f], add, state[:, j, f, 0:1],
                                                     ALU.mult, ALU.add)
                ins.then_inc(v_ab, 1)

            def wkv_new(b):
                dve.wait_ge(a_ex, 2 * b + 2)
                need(dve, v_atl, b)
                need(dve, a_ath, b)
                dve.tensor_tensor(n2, ex[:, 3], bankB[:], ALU.mult).then_inc(v_n2, 1)

            def wkv_old(b):
                dve.wait_ge(v_ab, b + 1)
                dve.tensor_tensor(n1, ex[:, 2], state[:, 1, :, 0:CT], ALU.mult).then_inc(v_n1, 1)

            def wkv_sum(b):
                dve.wait_ge(v_n1, b + 1)
                dve.tensor_tensor(n1, n1, n2, ALU.add).then_inc(v_n, 1)

            def wkv_sigmoid(b):
                dve.wait_ge(v_n, b + 1)
                dve.wait_ge(g_dn, b + 1)
                dve.wait_ge(a_er, b + 1)
                dve.scalar_tensor_tensor(n2, er, 1.0, kv_m, ALU.add, ALU.mult).then_inc(v_de, 1)

            def wkv_reciprocal(b, f):
                dve.wait_ge(v_de, b + 1)
                dve.reciprocal(kv_m[:, f], n2[:, f]).then_inc(v_rc, 1)

            def wkv_ratio(b):
                dve.wait_ge(v_rc, KC * (b + 1))
                dve.tensor_tensor(n1, n1, kv_m, ALU.mult).then_inc(v_at, 1)

            def mix_whole(src, j, name, free, done):
                for s, v in free:
                    need(dve, s, v)
                for f in range(KC):
                    ins = dve.scalar_tensor_tensor(xm[:, j % 2, f * CT:(f + 1) * CT], dx[:, f], pcol(name, f),
                                                   src[:, f, 0:CT], ALU.mult, ALU.add)
                ins.then_inc(done, 1)

            def mix_lo(operand, c, j, per, whole, hi, done):
                dve.wait_ge(whole, upto(per, j, c + 1))
                dve.wait_ge(hi, upto(per, j, c + 1))
                lo(operand[1][:, j], xm[:, j % 2].rearrange("p (a b) -> p a b", a=2), operand[0][:, j]).then_inc(done, 1)

            def cmix_whole(c, j):
                n = upto(3, 2 - j, c + 1)
                mix_whole(xn2, j, ("cmr", "cmk")[j], [(v_xml, n), (a_xmh, n)], v_cm)

            def tmix_whole(b, j):
                if j < 2:
                    free = [(v_cml, upto(2, j, b)), (a_cmh, upto(2, j, b))]
                else:
                    free = [(v_xml, upto(3, 0, b + 1)), (a_xmh, upto(3, 0, b + 1))]
                mix_whole(xn1, j, ("tmk", "tmv", "tmr")[j], free, v_xm)

            def iteration(it, A, B, C_, D):
                a, b, c, d = it, it - 1, it - 2, it - 3
                first = B and not C_
                if A:
                    dve.wait_ge(s_x, 16 * (a + 1))
                    stats(0, a, x_in)
                if D:
                    product(("C", 2), d, it - 1)
                if C_:
                    dve.wait_ge(a_xn2, c + 1)
                    need(dve, v_xm, upto(3, 2, c + 1))
                    dve.tensor_tensor(dx, xn2[:, :, 1:CT + 1], xn2[:, :, 0:CT], ALU.subtract).then_inc(v_dx2, 1)
                    dve.wait_ge(v_dx2, c + 1)
                    cmix_whole(c, 0)
                    cmix_whole(c, 1)
                    mix_lo(cmix, c, 0, 2, v_cm, a_cmh, v_cml)
                    mix_lo(cmix, c, 1, 2, v_cm, a_cmh, v_cml)
                if D:
                    dve.wait_ge(p_dn[1], d + 1)
                    need(dve, s_out, 16 * d)
                    dve.scalar_tensor_tensor(out_sb, bankC[:], 0.5, x3, ALU.mult, ALU.add).then_inc(v_out, 1)
                if B:
                    dve.wait_ge(a_xn1, b + 1)
                    need(dve, v_cm, upto(2, 1, b))
                    dve.tensor_tensor(dx, xn1[:, :, 1:CT + 1], xn1[:, :, 0:CT], ALU.subtract).then_inc(v_dx1, 1)
                    dve.wait_ge(v_dx1, b + 1)
                    tmix_whole(b, 0)
                if C_:
                    relu_square(c, 0, it)
                if B:
                    tmix_whole(b, 1)
                    mix_lo(mix, b, 0, 3, v_xm, a_xmh, v_xml)
                if C_:
                    relu_square(c, 1, it)
                if A:
                    dve.wait_ge(a_zh[0], a + 1)
                    lo(z0[1][:], bankT[:], z0[0][:]).then_inc(v_zl[0], 1)
                if B:
                    mix_lo(mix, b, 1, 3, v_xm, a_xmh, v_xml)
                    tmix_whole(b, 2)
                if C_:
                    relu_square(c, 2, it)
                if B:
                    mix_lo(mix, b, 2, 3, v_xm, a_xmh, v_xml)
                if C_:
                    relu_square(c, 3, it)
                if B:
                    wkv_state(b)
                if A and not first:
                    product(("A", 0), a, it)
                if B:
                    wkv_scans(b)
                if C_:
                    dve.wait_ge(p_cv, c + 1)
                    dve.scalar_tensor_tensor(th, th, 1.0, bankA[:], ALU.add, ALU.mult).then_inc(v_t3, 1)
                if B:
                    wkv_new(b)
                if C_:
                    dve.wait_ge(v_t3, c + 1)
                    dve.wait_ge(g_x12, c + 1)
                    need(dve, v_out, d + 1)
                    dve.scalar_tensor_tensor(x3, th, 0.5, x12, ALU.mult, ALU.add).then_inc(v_x3, 1)
                    dve.wait_ge(v_x3, c + 1)
                    stats(3, c, x3)
                if B:
                    wkv_old(b)
                if A and not first:
                    product(("A", 1), a, it)
                if B:
                    wkv_sum(b)
                if first:
                    product(("A", 0), a, it)
                if B:
                    wkv_sigmoid(b)
                    wkv_reciprocal(b, 0)
                if C_:
                    dve.wait_ge(a_zh[3], c + 1)
                    lo(z3[1][:], bankT[:], z3[0][:]).then_inc(v_zl[3], 1)
                if A:
                    product(("A", 1 if first else 2), a, it)
                if B:
                    wkv_reciprocal(b, 1)
                    wkv_ratio(b)
                if first:
                    product(("A", 2), a, it)
                if B:
                    dve.wait_ge(a_ath, b + 1)
                    lo(att[1][:], n1, att[0][:]).then_inc(v_atl, 1)
                if C_:
                    product(("C", 0), c, it)
                if A and not first:
                    residual(a)
                if B:
                    dve.wait_ge(p_wo, b + 1)
                    dve.wait_ge(g_y, b + 1)
                    need(dve, g_x12, c + 1)
                    dve.tensor_tensor(x2, bankA[:], y, ALU.add).then_inc(v_x2, 1)
                    dve.wait_ge(v_x2, b + 1)
                    stats(2, b, x2)
                if first:
                    residual(a)
                if A:
                    dve.wait_ge(v_x1, a + 1)
                    stats(1, a, x1)
                if C_:
                    product(("C", 1), c, it)

            prologue()

            def before():
                dve.wait_ge(s_x, 16)
                stats(0, 0, x_in)

            def after():
                dve.wait_ge(a_zh[0], 1)
                lo(z0[1][:], bankT[:], z0[0][:]).then_inc(v_zl[0], 1)

            decode(before, after)
            constants()
            clear()
            split_squares(POOL_SQ, POOL_SQ + 1)
            residual(0)
            dve.wait_ge(v_x1, 1)
            stats(1, 0, x1)
            split_squares(POOL_SQ + 1, NSQ)
            iteration(1, True, True, False, False)
            iteration(2, True, True, True, False)
            iteration(3, True, True, True, True)
            with dve.Fori(LOOP0, LOOP1) as it:
                iteration(it, True, True, True, True)
            iteration(NC, False, True, True, True)
            iteration(NC + 1, False, False, True, True)
            iteration(NC + 2, False, False, False, True)

        @block.gpsimd
        def _(pool):
            def rsqrt(k, c):
                pool.wait_ge(v_mv[k], c + 1)
                need(pool, a_z[k], c)
                pool.tensor_tensor(veps[:, k], mv[:, k, :, 1], eps[:], ALU.add).then_inc(g_ve[k], 1)
                pool.tensor_tensor(nmean[:, k], mv[:, k, :, 0], minus[:], ALU.mult).then_inc(g_mr[k], 1)
                pool.wait_ge(g_ve[k], c + 1)
                pool.tensor_tensor(rstd[:, k], veps[:, k], mhalf[:], ALU.pow).then_inc(g_pw[k], 1)
                pool.wait_ge(g_pw[k], c + 1)
                pool.wait_ge(g_mr[k], c + 1)
                pool.tensor_tensor(nbias[:, k], nmean[:, k], rstd[:, k], ALU.mult).then_inc(g_rs[k], 1)

            def rsqrt_double(c):
                var, mean = mv[:, 1, :, 1], mv[:, 1, :, 0]
                pool.wait_ge(v_mv[1], c + 1)
                need(pool, a_z[1], c)
                need(pool, g_y, c)
                pool.tensor_tensor(veps2[:, 0], var, eps[:], ALU.add).then_inc(g_ve[1], 1)
                pool.tensor_tensor(nmean[:, 1], mean, minus[:], ALU.mult).then_inc(g_mr[1], 1)
                pool.wait_ge(g_ve[1], 3 * c + 1)
                pool.tensor_tensor(veps2[:, 1], veps2[:, 0], eps[:], ALU.mult).then_inc(g_ve[1], 1)
                pool.wait_ge(g_ve[1], 3 * c + 2)
                pool.tensor_tensor(veps2[:, 1], veps2[:, 1], var, ALU.add).then_inc(g_ve[1], 1)
                pool.wait_ge(g_ve[1], 3 * c + 3)
                pool.tensor_tensor(scale2[:], veps2[:], mhalf[:].unsqueeze(1).to_broadcast([P, 2, TT]), ALU.pow).then_inc(g_pw[1], 1)
                pool.wait_ge(g_pw[1], c + 1)
                pool.wait_ge(g_mr[1], c + 1)
                pool.tensor_tensor(shift2[:], scale2[:], nmean[:, 1:2].to_broadcast([P, 2, TT]), ALU.mult).then_inc(g_rs[1], 1)

            def hidden_lo(tile, c):
                stage, p = tile
                ready, per = {"A": (a_hh[0], IP), "C": (a_hh[1], IP), "M": (a_h2h, HP)}[stage]
                pool.wait_ge(ready, upto(per, p, c + 1))
                whole = hval[:, SLOTS[TILES.index(tile)]].rearrange("p (a b) -> p a b", a=2)
                pool.tensor_tensor(hid[1][:, hid_pair(tile)], whole, hid[0][:, hid_pair(tile)].bitcast(F32),
                                   ALU.subtract).then_inc(lo_of(stage, p, 1)[0], 1)

            def decode():
                def leaves_of(n):
                    cols = slices[n][2]
                    pool.wait_ge(v_bit, n + 1)
                    need(pool, v_sel, 3 * (n - 1))
                    for j in range(ACT_LEAVES, 8):
                        ins = pool.tensor_scalar(leaves[n % 2][:, j, 0:2 * cols], bit0[n % 2][:, 0:2 * cols],
                                                 lutd[:, j:j + 1], lutb[:, 2 * j:2 * j + 1], ALU.mult, ALU.add)
                    ins.then_inc(g_leaf, 1)

                leaves_of(0)
                rsqrt(0, 0)
                leaves_of(1)
                for n in range(NSL - 1):
                    _, parts, cols, _ = slices[n]
                    pool.wait_ge(a_whi, n + 1)
                    for (hi, c0, c1), (lo_, _, _) in parts:
                        ins = pool.tensor_tensor(lo_, two(leaves[n % 2][:, 0], cols, c0, c1), hi.bitcast(F32), ALU.subtract)
                    ins.then_inc(g_wlo, 1)
                    if n + 2 < NSL:
                        leaves_of(n + 2)
                    if n in BETWEEN:
                        hidden_lo(("A", BETWEEN[n]), 0)

            def split_raws(n0, n1):
                for n in range(n0, n1):
                    raw, hi, lo_ = raws[n]
                    pool.wait_ge(a_raw, n + 1)
                    pool.tensor_tensor(lo_, raw, hi.bitcast(F32), ALU.subtract).then_inc(g_raw, 1)

            def iteration(it, A, B, C_, D):
                a, b, c, d = it, it - 1, it - 2, it - 3
                first = B and not C_
                if D:
                    hidden_lo(("C", 2), d)
                if A:
                    rsqrt(0, a)
                if C_:
                    for g in range(HP):
                        hidden_lo(("M", g), c)
                    pool.wait_ge(v_x2, c + 1)
                    need(pool, v_x3, c)
                    pool.tensor_tensor(x12, x2, x1k, ALU.add).then_inc(g_x12, 1)
                if B:
                    before = c + 1 if isinstance(it, int) else pool.snap(c + 1)
                    pool.wait_ge(g_ident, 2)
                    need(pool, g_x12, before)
                    pool.tensor_scalar(x1k, x1[:], 1.0, 0.0, ALU.mult, ALU.add).then_inc(g_x1k, 1)
                    pool.wait_ge(g_ident, 2)
                    need(pool, v_x2, before)
                    for t in range(TT):
                        ins = pool.tensor_scalar(y[:, t], x1[:, t], scale2[:, 0, t:t + 1], shift2[:, 0, t:t + 1],
                                                 ALU.mult, ALU.add)
                    ins.then_inc(g_y, 1)
                    if first:
                        split_raws(NSQ, NRAW)
                    if A and not first:
                        hidden_lo(("A", 0), a)
                    pool.wait_ge(v_ab, b + 1)
                    pool.wait_ge(a_ex, 2 * b + 2)
                    pool.tensor_tensor(kv_m, ex[:, 2], state[:, 2, :, 0:CT], ALU.mult).then_inc(g_d1, 1)
                    pool.wait_ge(g_d1, b + 1)
                    pool.tensor_tensor(kv_m, kv_m, ex[:, 3], ALU.add).then_inc(g_dn, 1)
                    if first:
                        hidden_lo(("A", 0), a)
                if C_:
                    rsqrt(3, c)
                if A:
                    hidden_lo(("A", 1), a)
                    hidden_lo(("A", 2), a)
                if C_:
                    hidden_lo(("C", 0), c)
                if B:
                    rsqrt(2, b)
                if A:
                    rsqrt_double(a)
                if C_:
                    hidden_lo(("C", 1), c)

            idx_last = idx_dn[:, KI - 1, :]
            pool.memset(idx_last, 0).then_inc(g_clear, 1)
            for const, value in ((mhalf, -0.5), (eps, EPS), (minus, -1.0)):
                pool.memset(const[:], value)
            for w in w_gate:
                pool.memset(w[:, :, I:IFULL + UPROW].bitcast(F32), 0.0)
            pool.memset(ident[:], 0.0).then_inc(g_ident, 1)
            pool.wait_ge(g_ident, 1)
            pool.affine_select(out=ident[:], in_=ident[:], compare_op=ALU.not_equal, fill=1.0, base=0,
                               pattern=[[-1, P]], channel_multiplier=1).then_inc(g_ident, 1)
            pool.wait_ge(v_lutd, 1)
            pool.wait_ge(g_ident, 2)
            decode()
            split_raws(0, POOL_SQ)
            rsqrt_double(0)
            pool.wait_ge(v_clear, 1)
            iteration(1, True, True, False, False)
            iteration(2, True, True, True, False)
            iteration(3, True, True, True, True)
            with pool.Fori(LOOP0, LOOP1) as it:
                iteration(it, True, True, True, True)
            iteration(NC, False, True, True, True)
            iteration(NC + 1, False, False, True, True)
            iteration(NC + 2, False, False, False, True)

        return nc


def kernel(**inputs):
    import numpy as np
    import concourse.bacc as bacc
    from concourse.bass_utils import run_bass_kernel_spmd

    def tiles(w):
        r, c = w.shape
        return np.ascontiguousarray(w.reshape(r // P, P, c).transpose(1, 0, 2))

    def get(name):
        return np.asarray(inputs["L0_" + name])

    params = np.stack([get("attn_" + n) for n in PARAMS]).reshape(len(PARAMS), KC, P).transpose(2, 0, 1)
    arrays = {
        "in_x": get("attn_x").reshape(T, C),
        "in_params": np.ascontiguousarray(params),
        "in_lut": np.ascontiguousarray(np.broadcast_to(get("ffn_lut"), (P, LUT))),
        "in_gate": tiles(get("ffn_gate_idx").T),
        "in_up": tiles(get("ffn_up_idx").T),
        "in_down": np.ascontiguousarray(get("ffn_down_idx").T),
        "in_square": np.ascontiguousarray(np.stack([tiles(get("attn_" + n).T) for n in SQUARE], axis=1)),
        "in_wck": tiles(get("attn_Wck").T),
        "in_wcv": tiles(get("attn_Wcv").T),
    }
    nc = bacc.Bacc("TRN2", target_bir_lowering=False, num_devices=1)
    args = [nc.dram_tensor(n, a.shape, mybir.dt.from_np(a.dtype), kind="ExternalInput").ap() for n, a in arrays.items()]
    out = nc.dram_tensor("out", (T, C), F32, kind="ExternalOutput").ap()
    build(nc, *args, out)
    r = run_bass_kernel_spmd(nc, [arrays], core_ids=[0])
    return r.results[0]["out"].reshape(1, T, C)
```
